# Optimizing a Trainium2 kernel written in Bass

```python
import numpy as np
import jax
import jax.numpy as jnp

def _softmax(x, axis=-1):
    return jax.nn.softmax(x, axis=axis)

def _gelu(x):
    return jax.nn.gelu(x, approximate=True)

def _silu(x):
    return jax.nn.silu(x)

def _sigmoid(x):
    return jax.nn.sigmoid(x)

def _layernorm(x, axis=-1, eps=1e-05):
    m = jnp.mean(x, axis=axis, keepdims=True)
    v = jnp.var(x, axis=axis, keepdims=True)
    return (x - m) / jnp.sqrt(v + eps)

def _scatter_add(tgt, idx, src, axis=0):
    return tgt.at[idx].add(src)

def _segment_sum(src, seg, n):
    return jax.ops.segment_sum(src, seg, n)
kernel_name = 'mk_seq_preln_d2_jaxref_r8_965f61'

def setup_inputs(seed: int=0):
    np.random.seed(seed)
    _w = jnp.asarray

    def _L0_attn_setup():
        import jax, jax.numpy as jnp
        import numpy as np
        BH = 32
        BW = 32
        key = jax.random.key(seed)
        k1, k2, k3, k4 = jax.random.split(key, 4)
        B, S, K, N = (2, 256, 512, 512)
        data = jax.random.normal(k1, (B, S, K), dtype=jnp.float32)
        weight = jax.random.normal(k2, (N, K), dtype=jnp.float32) * 0.02
        bias = jax.random.normal(k3, (N,), dtype=jnp.float32) * 0.02
        Nb, Kb = (N // BH, K // BW)
        block_on = jax.random.uniform(k4, (Nb, Kb)) < 0.3
        mask = jnp.repeat(jnp.repeat(block_on, BH, axis=0), BW, axis=1).astype(jnp.int32)
        return {'data': data, 'mask': mask, 'weight': weight, 'bias': bias}
    _L0_attn_in = _L0_attn_setup()

    def _L0_ffn_setup():
        import jax, jax.numpy as jnp
        import numpy as np
        GROUP = 64

        def dequant_q40(w, s, out_features, in_features):
            msb = w >> 4
            lsb = (w & 15 ^ 8) - 8
            g = jnp.concatenate([msb, lsb], axis=1).reshape(-1, GROUP)
            deq = g.astype(s.dtype) * s[:, None]
            return deq.reshape(out_features, in_features)
        key = jax.random.key(seed)
        ks = jax.random.split(key, 7)
        dim, hidden = (512, 1376)
        B, S = (2, 256)

        def packed(k, din, dout):
            return jax.random.randint(k, (din * dout // GROUP // 2, GROUP), -128, 128, dtype=jnp.int32)

        def scales(k, din, dout):
            return (jax.random.uniform(k, (din * dout // GROUP,), dtype=jnp.float32) + 0.5) * 0.01
        x = jax.random.normal(ks[0], (B, S, dim), dtype=jnp.float32)
        w1 = packed(ks[1], dim, hidden)
        s1 = scales(ks[2], dim, hidden)
        w2 = packed(ks[3], hidden, dim)
        s2 = scales(ks[4], hidden, dim)
        w3 = packed(ks[5], dim, hidden)
        s3 = scales(ks[6], dim, hidden)
        return {'x': x, 'w1': w1, 's1': s1, 'w2': w2, 's2': s2, 'w3': w3, 's3': s3}
    _L0_ffn_in = _L0_ffn_setup()

    def _L1_attn_setup():
        import jax, jax.numpy as jnp
        import numpy as np
        HIDDEN = 512
        N_HEADS = 32
        N_KV_HEADS = 8
        HEAD_DIM = HIDDEN // N_HEADS
        N_REP = N_HEADS // N_KV_HEADS
        KV_DIM = N_KV_HEADS * HEAD_DIM

        def _kaiming_uniform(key, out_f, in_f):
            bound = 1.0 / np.sqrt(in_f)
            return jax.random.uniform(key, (out_f, in_f), jnp.float32, -bound, bound)

        def bitnet_linear(x, weight, scale_param):
            s = jnp.maximum(jnp.mean(jnp.abs(weight), axis=1), 1e-08)
            binary_w = jnp.sign(weight / s[:, None])
            y = jnp.einsum('bsi,oi->bso', x, binary_w)
            y = y * (s * scale_param)[None, None, :]
            return jnp.nan_to_num(y, nan=0.0, posinf=1000000.0, neginf=-1000000.0)
        key = jax.random.key(seed)
        ks = jax.random.split(key, 5)
        return {'hidden_states': jax.random.normal(ks[0], (1, 256, HIDDEN), jnp.float32), 'q_weight': _kaiming_uniform(ks[1], HIDDEN, HIDDEN), 'q_scale': jnp.ones((HIDDEN,), jnp.float32), 'k_weight': _kaiming_uniform(ks[2], KV_DIM, HIDDEN), 'k_scale': jnp.ones((KV_DIM,), jnp.float32), 'v_weight': _kaiming_uniform(ks[3], KV_DIM, HIDDEN), 'v_scale': jnp.ones((KV_DIM,), jnp.float32), 'o_weight': _kaiming_uniform(ks[4], HIDDEN, HIDDEN), 'o_scale': jnp.ones((HIDDEN,), jnp.float32)}
    _L1_attn_in = _L1_attn_setup()

    def _L1_ffn_setup():
        import jax, jax.numpy as jnp
        import numpy as np

        @jax.custom_vjp
        def ste_sign(w):
            return jnp.sign(w)

        def _ste_fwd(w):
            return (jnp.sign(w), w)

        def _ste_bwd(w, g):
            mask = ((w > -1) & (w < 1)).astype(g.dtype)
            return (g * mask,)
        ste_sign.defvjp(_ste_fwd, _ste_bwd)
        key = jax.random.key(seed)
        k = jax.random.split(key, 6)
        B, S, H, O, E = (4, 256, 512, 512, 8)
        return {'x': jax.random.normal(k[0], (B, S, H), dtype=jnp.float32), 'weight': jax.random.normal(k[1], (O, H), dtype=jnp.float32) * 0.02, 'bias': jax.random.normal(k[2], (O,), dtype=jnp.float32) * 0.02, 'gate_w': jax.random.normal(k[3], (E, H), dtype=jnp.float32) * 0.02, 'in_channel_scale': jax.random.normal(k[4], (E, H), dtype=jnp.float32), 'out_channel_scale': jax.random.normal(k[5], (E, O), dtype=jnp.float32)}
    _L1_ffn_in = _L1_ffn_setup()
    _d = {'L0_attn_data': _L0_attn_in['data'], 'L0_attn_mask': _L0_attn_in['mask'], 'L0_attn_weight': _L0_attn_in['weight'], 'L0_attn_bias': _L0_attn_in['bias'], 'L0_ffn_w1': _L0_ffn_in['w1'], 'L0_ffn_s1': _L0_ffn_in['s1'], 'L0_ffn_w2': _L0_ffn_in['w2'], 'L0_ffn_s2': _L0_ffn_in['s2'], 'L0_ffn_w3': _L0_ffn_in['w3'], 'L0_ffn_s3': _L0_ffn_in['s3'], 'L1_attn_q_weight': _L1_attn_in['q_weight'], 'L1_attn_q_scale': _L1_attn_in['q_scale'], 'L1_attn_k_weight': _L1_attn_in['k_weight'], 'L1_attn_k_scale': _L1_attn_in['k_scale'], 'L1_attn_v_weight': _L1_attn_in['v_weight'], 'L1_attn_v_scale': _L1_attn_in['v_scale'], 'L1_attn_o_weight': _L1_attn_in['o_weight'], 'L1_attn_o_scale': _L1_attn_in['o_scale'], 'L1_ffn_weight': _L1_ffn_in['weight'], 'L1_ffn_bias': _L1_ffn_in['bias'], 'L1_ffn_gate_w': _L1_ffn_in['gate_w'], 'L1_ffn_in_channel_scale': _L1_ffn_in['in_channel_scale'], 'L1_ffn_out_channel_scale': _L1_ffn_in['out_channel_scale']}
    _x0 = _d['L0_attn_data']
    _d['L0_attn_data'] = jax.random.normal(jax.random.fold_in(jax.random.key(seed), 1), (1, 1024, 512), dtype=_x0.dtype)
    del _x0
    return _d

def reference(L0_attn_data, L0_attn_mask, L0_attn_weight, L0_attn_bias, L0_ffn_w1, L0_ffn_s1, L0_ffn_w2, L0_ffn_s2, L0_ffn_w3, L0_ffn_s3, L1_attn_q_weight, L1_attn_q_scale, L1_attn_k_weight, L1_attn_k_scale, L1_attn_v_weight, L1_attn_v_scale, L1_attn_o_weight, L1_attn_o_scale, L1_ffn_weight, L1_ffn_bias, L1_ffn_gate_w, L1_ffn_in_channel_scale, L1_ffn_out_channel_scale):

    def _L0_attn_ref(data, mask, weight, bias):
        import jax, jax.numpy as jnp
        import numpy as np
        BH = 32
        BW = 32
        N, K = weight.shape
        Nb, Kb = (N // BH, K // BW)
        bm = mask.reshape(Nb, BH, Kb, BW).sum(axis=(1, 3)) > 0
        wb = weight.reshape(Nb, BH, Kb, BW) * bm[:, None, :, None].astype(weight.dtype)
        w = wb.reshape(N, K)
        out = jnp.einsum('bsk,nk->bsn', data, w) + bias
        return out

    def _L0_ffn_ref(x, w1, s1, w2, s2, w3, s3):
        import jax, jax.numpy as jnp
        import numpy as np
        GROUP = 64

        def dequant_q40(w, s, out_features, in_features):
            msb = w >> 4
            lsb = (w & 15 ^ 8) - 8
            g = jnp.concatenate([msb, lsb], axis=1).reshape(-1, GROUP)
            deq = g.astype(s.dtype) * s[:, None]
            return deq.reshape(out_features, in_features)
        dim = x.shape[-1]
        hidden = w1.shape[0] * w1.shape[1] * 2 // dim
        W1 = dequant_q40(w1, s1, hidden, dim)
        W3 = dequant_q40(w3, s3, hidden, dim)
        W2 = dequant_q40(w2, s2, dim, hidden)
        a = jnp.einsum('bsd,hd->bsh', x, W1)
        b = jnp.einsum('bsd,hd->bsh', x, W3)
        h = jax.nn.silu(a) * b
        return jnp.einsum('bsh,dh->bsd', h, W2)

    def _L1_attn_ref(hidden_states, q_weight, q_scale, k_weight, k_scale, v_weight, v_scale, o_weight, o_scale):
        import jax, jax.numpy as jnp
        import numpy as np
        HIDDEN = 512
        N_HEADS = 32
        N_KV_HEADS = 8
        HEAD_DIM = HIDDEN // N_HEADS
        N_REP = N_HEADS // N_KV_HEADS
        KV_DIM = N_KV_HEADS * HEAD_DIM

        def _kaiming_uniform(key, out_f, in_f):
            bound = 1.0 / np.sqrt(in_f)
            return jax.random.uniform(key, (out_f, in_f), jnp.float32, -bound, bound)

        def bitnet_linear(x, weight, scale_param):
            s = jnp.maximum(jnp.mean(jnp.abs(weight), axis=1), 1e-08)
            binary_w = jnp.sign(weight / s[:, None])
            y = jnp.einsum('bsi,oi->bso', x, binary_w)
            y = y * (s * scale_param)[None, None, :]
            return jnp.nan_to_num(y, nan=0.0, posinf=1000000.0, neginf=-1000000.0)
        b, s, _ = hidden_states.shape
        q = bitnet_linear(hidden_states, q_weight, q_scale)
        k = bitnet_linear(hidden_states, k_weight, k_scale)
        v = bitnet_linear(hidden_states, v_weight, v_scale)
        q = q.reshape(b, s, N_HEADS, HEAD_DIM).transpose(0, 2, 1, 3)
        k = k.reshape(b, s, N_KV_HEADS, HEAD_DIM).transpose(0, 2, 1, 3)
        v = v.reshape(b, s, N_KV_HEADS, HEAD_DIM).transpose(0, 2, 1, 3)
        k = jnp.repeat(k, N_REP, axis=1)
        v = jnp.repeat(v, N_REP, axis=1)
        scores = jnp.einsum('bhqd,bhkd->bhqk', q, k) / np.sqrt(HEAD_DIM)
        attn = jax.nn.softmax(scores, axis=-1)
        out = jnp.einsum('bhqk,bhkd->bhqd', attn, v)
        out = out.transpose(0, 2, 1, 3).reshape(b, s, HIDDEN)
        return bitnet_linear(out, o_weight, o_scale)

    def _L1_ffn_ref(x, weight, bias, gate_w, in_channel_scale, out_channel_scale):
        import jax, jax.numpy as jnp
        import numpy as np

        @jax.custom_vjp
        def ste_sign(w):
            return jnp.sign(w)

        def _ste_fwd(w):
            return (jnp.sign(w), w)

        def _ste_bwd(w, g):
            mask = ((w > -1) & (w < 1)).astype(g.dtype)
            return (g * mask,)
        ste_sign.defvjp(_ste_fwd, _ste_bwd)
        B, S, H = x.shape
        xf = x.reshape(-1, H)
        router_logits = xf @ gate_w.T
        routing = jax.nn.softmax(router_logits.astype(jnp.float32), axis=1).astype(x.dtype)
        in_scale = routing @ in_channel_scale
        out_scale = routing @ out_channel_scale
        wb = ste_sign(weight)
        out = xf * in_scale @ wb.T * out_scale + bias
        return out.reshape(B, S, -1)
    x = L0_attn_data
    x = x + _L0_attn_ref(_layernorm(x, axis=-1), L0_attn_mask, L0_attn_weight, L0_attn_bias)
    x = x + _L0_ffn_ref(_layernorm(x, axis=-1), L0_ffn_w1, L0_ffn_s1, L0_ffn_w2, L0_ffn_s2, L0_ffn_w3, L0_ffn_s3)
    x = x + _L1_attn_ref(_layernorm(x, axis=-1), L1_attn_q_weight, L1_attn_q_scale, L1_attn_k_weight, L1_attn_k_scale, L1_attn_v_weight, L1_attn_v_scale, L1_attn_o_weight, L1_attn_o_scale)
    x = x + _L1_ffn_ref(_layernorm(x, axis=-1), L1_ffn_weight, L1_ffn_bias, L1_ffn_gate_w, L1_ffn_in_channel_scale, L1_ffn_out_channel_scale)
    return x

_drawn_inputs = setup_inputs


def setup_inputs(seed=0):
    import zlib

    import numpy as np

    out = dict(_drawn_inputs(seed))
    spreads = {'L1_attn_q_scale': (1.0, 0.6),
     'L1_attn_k_scale': (1.0, 0.6),
     'L1_attn_v_scale': (1.0, 0.6),
     'L1_attn_o_scale': (1.0, 0.6)}
    factors = {'L1_attn_q_weight': 8.0,
     'L1_attn_k_weight': 8.0,
     'L1_attn_v_weight': 5.596,
     'L1_attn_o_weight': 5.733,
     'L1_ffn_bias': 53.53}
    for name, (base, spread) in spreads.items():
        noise = np.random.default_rng([zlib.crc32(name.encode()), seed]).standard_normal(out[name].shape)
        drawn = base * np.exp(spread * noise) if base else spread * noise
        out[name] = jnp.asarray(drawn.astype(out[name].dtype))
    for name, factor in factors.items():
        out[name] = (out[name] * factor).astype(out[name].dtype)
    return out
```

```python
from contextlib import ExitStack

import concourse.bass as bass
from concourse import mybir

F32 = mybir.dt.float32
F32R = mybir.dt.float32r
BF16 = mybir.dt.bfloat16
I32 = mybir.dt.int32
ALU = mybir.AluOpType
ACT = mybir.ActivationFunctionType
AX = mybir.AxisListType.X

P = 128
TOK, DIM, HID = 1024, 512, 1376
TT = TOK // P
KT = DIM // P
HT = -(-HID // P)
HALVES = (0, 6, HT)
CH = 2
HEADS, KVH, HD = 32, 8, 16
REP = HEADS // KVH
EXP = 8
EPS = 1e-5
NTERM = 6
Q_PART = (0, 0, 0, 1, 1, 2)
K_PART = (0, 1, 2, 0, 1, 0)
SROWS = NTERM * HD
MROWS = SROWS + 3
FULL = 3.4028235e38
STEPS = CH * TT
MAXT = REP * TT
MAXSTEPS = 14


def build(nc, A, out):
    with ExitStack() as ctx:
        sems = {}

        def sem(name):
            if name not in sems:
                sems[name] = ctx.enter_context(nc.semaphore(name))
            return sems[name]

        base = (nc.sbuf_base + 63) // 64 * 64
        size = {F32: 4, F32R: 4, BF16: 2, I32: 4}
        end = nc.sbuf_usable_end

        class Region:
            def __init__(self, start):
                self.at = start

            def __call__(self, name, shape, dt):
                n = size[dt]
                for s in shape[1:]:
                    n *= s
                t = nc.alloc_sbuf_tensor_at("sb_" + name, list(shape), dt, offset=self.at)
                self.at += -(-n // 32) * 32
                assert self.at <= end, (name, self.at, end)
                return t

        keep = Region(base)
        X = keep("X", [P, TT, DIM], F32)
        ID = keep("ID", [P, P], F32)
        IDB = keep("IDB", [P, P], BF16)
        ONES = keep("ONES", [P, P], F32)
        BLK = keep("BLK", [P, P], F32)
        ST = keep("ST", [P, TT, 6], F32)
        MV = keep("MV", [P, TT, 2], F32)
        RSTD = keep("RSTD", [P, TT], F32)
        NHALF = keep("NHALF", [P, TT], F32)
        SQK = keep("SQK", [P, 5], F32)
        QKSC = keep("QKSC", [P, 5], F32)
        SVB = keep("SVB", [P, P], F32)
        VSC = keep("VSC", [P, P], F32)
        BIAS0 = keep("BIAS0", [P, DIM], F32)
        SH2 = keep("SH2", [P, 4, 2], I32)
        xnh_at = keep.at
        XNH = keep("XNH", [P, KT, TOK], F32R)
        xnl_at = keep.at
        XNL = keep("XNL", [P, KT, TOK], F32R)
        xn_at = keep.at
        XN = keep("XN", [P, 3, DIM], F32)
        SGQ = keep("SGQ", [P, KT, DIM], F32R)
        SGKV = keep("SGKV", [P, KT, 2 * P], F32R)
        arena = keep.at
        ra = Region(arena)
        W0 = ra("W0", [P, KT, DIM], F32)
        M0 = ra("M0", [P, KT, DIM], I32)
        W0H = ra("W0H", [P, KT, DIM], F32R)
        W0L = ra("W0L", [P, KT, DIM], F32R)
        RAW = ra("RAW", [P, 2, DIM], F32)
        ABS = ra("ABS", [P, 2, DIM], F32)
        BSUM = ra("BSUM", [P, KT * 16], F32)
        BON = ra("BON", [P, KT * 16], F32)
        rf = Region(arena)
        HH = rf("HH", [P, HALVES[1], TOK], F32R)
        HL = rf("HL", [P, HALVES[1], TOK], F32R)
        W2H = rf("W2H", [P, HALVES[1], DIM], F32R)
        W2L = rf("W2L", [P, HALVES[1], DIM], F32R)
        WH = rf("WH", [P, 2, 2, KT, P], F32R)
        WL = rf("WL", [P, 2, 2, KT, P], F32R)
        P13 = rf("P13", [P, 2, 4, P], I32)
        S13 = rf("S13", [P, 2, 8, P], F32)
        N13 = rf("N13", [P, 8, P], I32)
        WF = rf("WF", [P, 8, P], F32)
        P2 = rf("P2", [P, 2, DIM], I32)
        S2 = rf("S2", [P, 2, DIM], F32)
        N2 = rf("N2", [P, DIM], I32)
        W2F = rf("W2F", [P, DIM], F32)
        TH = rf("TH", [P, 2, DIM], F32)
        UU = rf("UU", [P, 2, DIM], F32)
        HF = rf("HF", [P, 2, DIM], F32)
        rt = Region(arena)
        QS = rt("QS", [P, HEADS, TOK], BF16)
        KS = rt("KS", [P, KVH, TOK], BF16)
        QP = rt("QP", [P, 4, 3, TOK], BF16)
        KP = rt("KP", [P, 3, TOK], BF16)
        V16 = rt("V16", [P, KVH, TT, HD], F32)
        VS = rt("VS", [P, 2, TT, 32], F32)
        MX = rt("MX", [P, 2, MAXT], F32)
        MR = rt("MR", [P, MAXT], F32)
        NM = rt("NM", [P, 2, 3, MAXT], BF16)
        MT = rt("MT", [3 * MAXT, 2, P], BF16)
        YS = rt("YS", [P, 2, DIM], F32)
        YP = rt("YP", [P, DIM], F32)
        YN = rt("YN", [P, DIM], F32)
        FIN = rt("FIN", [P, DIM], F32)
        rp = Region(xnh_at)
        PR = rp("PR", [P, 2, REP, DIM], F32)
        OT0 = rp("OT0", [P, KVH, DIM], F32)
        OT1 = rp("OT1", [P, KVH, DIM], F32)
        OT = (OT0, OT1)
        assert rp.at <= arena
        re = Region(arena)
        SGO = re("SGO", [P, KT, DIM], F32R)
        SGF = re("SGF", [P, KT, DIM], F32R)
        RAWO = re("RAWO", [P, KT, DIM], F32)
        RAWF = re("RAWF", [P, KT, DIM], F32)
        ABSO = re("ABSO", [P, KT, DIM], F32)
        SOB = re("SOB", [P, DIM], F32)
        OSC = re("OSC", [P, DIM], F32)
        BIASF = re("BIASF", [P, DIM], F32)
        GATE = re("GATE", [P, KT, EXP], F32)
        GTH = re("GTH", [P, KT, EXP], F32R)
        GTL = re("GTL", [P, KT, EXP], F32R)
        CS = re("CS", [EXP, 2 * DIM], F32)
        CSH = re("CSH", [EXP, 2 * DIM], F32R)
        CSL = re("CSL", [EXP, 2 * DIM], F32)
        CSA = re("CSA", [3 * EXP, 2 * DIM], F32)
        CSS = re("CSS", [3 * EXP, 2 * DIM], F32R)
        ON = re("ON", [P, 2, DIM], F32)
        XE = re("XE", [P, 4, DIM], F32)
        ZI = re("ZI", [P, 2, DIM], F32)
        EH = re("EH", [P, 3, 2, KT, P], F32R)
        EL = re("EL", [P, 3, 2, KT, P], F32R)
        DEN = re("DEN", [P, HEADS], F32)
        EYS = re("EYS", [P, DIM], F32)
        EYP = re("EYP", [P, DIM], F32)
        EYN = re("EYN", [P, DIM], F32)
        EFIN = re("EFIN", [P, DIM], F32)
        RM = re("RM", [P, 4], F32)
        RE = re("RE", [P, EXP], F32)
        RF = re("RF", [P, EXP], F32)
        RH = re("RH", [P, EXP], F32R)
        RL = re("RL", [P, 3 * EXP], F32)
        RT = re("RT", [3 * EXP, P], F32R)
        OS = re("OS", [P, 3, DIM], F32)
        ZO = re("ZO", [P, 2, DIM], F32)

        PS = ctx.enter_context(nc.psum_tensor("PS", [P, 8, DIM], F32))

        f32 = lambda ap: ap.bitcast(F32)

        order = [(1, 0), (1, 1)]
        for t in range(TT):
            if t >= 1:
                order.append((2, t - 1))
            if t + 2 < TT:
                order.append((1, t + 2))
        order.append((2, TT - 1))
        seq = {k: n for n, k in enumerate(order)}
        NA = len(order)
        block = ctx.enter_context(nc.Block())

        def half_of(h):
            return 0 if h < HALVES[1] else 1

        def transpose3(pe, t):
            pe.wait_ge(sem("xn3_done"), t + 1)
            if t >= 2:
                pe.wait_ge(sem("xnl3_done"), t - 1)
            for k in range(KT):
                ins = pe.transpose(PS[:, 2 + t % 2, P * k:P * k + P], XN[:, t % 3, P * k:P * k + P], ID[:])
            ins.then_inc(sem("tr3_done"), 1)

        @block.sync
        def _(sp):
            sp.dma_start(X[:], A["x"]).then_inc(sem("x_loaded"), 16)
            sp.dma_start(M0[:], A["m0"]).then_inc(sem("w0_loaded"), 16)
            sp.dma_start(W0[:], A["w0"]).then_inc(sem("w0_loaded"), 16)
            for dst, src in ((BLK[:], "blk"), (ID[:], "ident"), (BIAS0[:], "bias0"), (ONES[:], "ones"),
                             (SH2[:], "sh2"), (QKSC[:], "qksc"),
                             (VSC[:], "vsc")):
                ap = A[src]
                if src in ("bias0", "vsc"):
                    ap = ap.broadcast_to([P, ap.shape[1]])
                sp.dma_start(dst, ap).then_inc(sem("consts_loaded"), 16)

            def load_hidden(h, par, first):
                if not first:
                    sp.wait_ge(sem("n13_done"), h - 1)
                    sp.wait_ge(sem("wf_done"), h - 1)
                sp.dma_start(P13[:, par], A["p13"][h]).then_inc(sem(f"p13_loaded{par}"), 16)
                for c in range(2):
                    sp.dma_start(S13[64 * c:64 * c + 64, par],
                                 A["s13"][h, c:c + 1].broadcast_to([64, 8, P])).then_inc(sem(f"p13_loaded{par}"), 16)
                if not first:
                    sp.wait_ge(sem("n2_done"), h - 1)
                    sp.wait_ge(sem("w2f_done"), h - 1)
                sp.dma_start(P2[:, par], A["p2"][h]).then_inc(sem(f"p2_loaded{par}"), 16)
                for b in range(4):
                    sp.dma_start(S2[32 * b:32 * b + 32, par],
                                 A["s2"][h, b:b + 1].broadcast_to([32, DIM])).then_inc(sem(f"p2_loaded{par}"), 16)

            for n in range(6):
                if n >= 2:
                    sp.wait_ge(sem("abs_done"), n - 1)
                sp.dma_start(RAW[:, n % 2], A["wqkv"][n]).then_inc(sem(f"raw_loaded{n % 2}"), 16)
            load_hidden(0, 0, True)
            load_hidden(1, 1, True)
            with sp.Fori(1, HT // 2) as i:
                for par in range(2):
                    load_hidden(i * 2 + par, par, False)
            load_hidden(HT - 1, (HT - 1) % 2, False)
            def load_ks(g):
                for r in range(NTERM):
                    sp.dma_start(KS[HD * r:HD * r + HD, g], KP[HD * g:HD * g + HD, K_PART[r]]).then_inc(
                        sem("ks0_loaded" if g == 0 else "ks_loaded"), 16)

            def load_qs(T, u):
                for j in range(REP):
                    for r in range(NTERM):
                        sp.dma_start(QS[HD * r:HD * r + HD, (2 * T + u) * REP + j],
                                     QP[HD * (u * REP + j):HD * (u * REP + j) + HD, T, Q_PART[r]]).then_inc(
                            sem("qs_loaded"), 16)
                sp.wait_ge(sem("qs_loaded"), 16 * REP * NTERM * (2 * T + u + 1))

            def load_m(g):
                sp.wait_ge(sem("mt_done"), g + 1)
                sp.dma_start(QS[SROWS:MROWS, REP * g:REP * g + REP].rearrange("p h (q c) -> p (h q) c", c=P),
                             MT[:, g % 2]).then_inc(sem("m_loaded"), 16)

            sp.wait_ge(sem("kp_done"), CH)
            load_ks(0)
            sp.wait_ge(sem("qp_done"), 5)
            load_qs(0, 0)
            for g in range(1, KVH):
                load_ks(g)
            load_m(0)
            load_qs(0, 1)
            for g in range(1, KVH):
                if g % 2 == 1 and g // 2 < 3:
                    sp.wait_ge(sem("qp_done"), 6 + g // 2)
                if g + 1 < KVH:
                    load_qs((g + 1) // 2, (g + 1) % 2)
                load_m(g)
            sp.wait_ge(sem("pv_done"), KVH * STEPS)
            for dst, src in ((RAWO[:], A["wo"]), (RAWF[:], A["wf"]), (OSC[:], A["osc"].broadcast_to([P, DIM])),
                             (BIASF[:], A["biasf"].broadcast_to([P, DIM])), (GATE[:], A["gate"]),
                             (CS[:], A["cs"])):
                sp.dma_start(dst, src).then_inc(sem("tail_loaded"), 16)
            sp.wait_ge(sem("cs_split"), 2)
            for e, src in enumerate((f32(CSH[:]), f32(CSH[:]), CSL[:])):
                sp.dma_start(CSA[EXP * e:EXP * e + EXP], src).then_inc(sem("css_loaded"), 16)
            for t in range(TT):
                sp.wait_ge(sem("zo_done"), t + 1)
                sp.dma_start(out[:, t], ZO[:, t % 2]).then_inc(sem(f"stored{t % 2}"), 16)
            for par in range(2):
                sp.wait_ge(sem(f"stored{par}"), 16 * (TT // 2))

        @block.gpsimd
        def _(pool):
            pool.memset(NHALF[:], -0.5).then_inc(sem("nhalf_done"), 1)
            pool.wait_ge(sem("nhalf_done"), 1)

            def rstd(sl, n_mv):
                pool.wait_ge(sem("mv_done"), n_mv)
                pool.tensor_tensor(RSTD[:, sl], MV[:, sl, 1], NHALF[:, sl], ALU.pow).then_inc(sem("rstd_done"), 1)

            rstd(slice(0, TT), 1)
            pool.wait_ge(sem("w0h_done"), 1)
            pool.tensor_tensor(W0L[:], W0[:], f32(W0H[:]), ALU.subtract).then_inc(sem("w0l_done"), 1)
            pool.wait_ge(sem("consts_loaded"), 16 * 7)
            for t in range(TT):
                pool.wait_ge(sem("xn_done"), seq[(1, t)] + 1)
                pool.tensor_tensor(X[:, t], X[:, t], BIAS0[:], ALU.add).then_inc(sem("bias_done"), 1)
                rstd(slice(t, t + 1), 2 + t)

            def prepare(h, par, first, slot):
                pool.wait_ge(sem("wh_done"), h + 1)
                pool.tensor_tensor(WL[:, par], WF[:].rearrange("p (w k) o -> p w k o", w=2), f32(WH[:, par]),
                                   ALU.subtract).then_inc(sem("wl_done"), 1)
                pool.wait_ge(sem("w2h_done"), h + 1)
                pool.tensor_tensor(W2L[:, slot], W2F[:], f32(W2H[:, slot]), ALU.subtract).then_inc(sem("w2l_done"), 1)

            prepare(0, 0, True, 0)
            for h in range(1, HT):
                prepare(h, h % 2, False, h - HALVES[half_of(h)])
            for t in range(TT):
                rstd(slice(t, t + 1), 2 + TT + t)
            pool.wait_ge(sem("proj_done"), 1)
            pool.wait_ge(sem("rstd_done"), 1 + 2 * TT)
            pool.memset(KS[SROWS:MROWS], 1.0).then_inc(sem("ks_ones"), 1)
            pool.wait_ge(sem("ks_ones"), 1)
            pool.memset(VS[:], 1.0).then_inc(sem("vs_ones"), 1)
            pool.wait_ge(sem("vs_ones"), 1)
            for u in range(12):
                c, i = u // 6, u % 6
                cs = slice(DIM * c, DIM * c + DIM)
                pool.wait_ge(sem("finite_done"), u + 1)
                if i == 1:
                    pool.tensor_copy(V16[:, :, 4 * c:4 * c + 4].rearrange("p g t d -> p t g d"),
                                     YP[:].rearrange("p (t g d) -> p t g d", t=4, g=KVH)).then_inc(sem("split_done"), 1)
                    continue
                parts = KP if i == 0 else QP[:, i - 2]
                pool.wait_ge(sem("part_hi"), u + 1)
                pool.tensor_tensor(YN[:], YP[:], parts[:, 0, cs], ALU.subtract).then_inc(sem("rest_done"), 1)
                pool.wait_ge(sem("part_mid"), u + 1)
                pool.tensor_tensor(parts[:, 2, cs], YN[:], parts[:, 1, cs], ALU.subtract).then_inc(
                    sem("split_done"), 1)
                pool.wait_ge(sem("split_done"), u + 1)
                pool.sem_inc(sem("kp_done") if i == 0 else sem("qp_done"), 1)

            pool.wait_ge(sem("vs_ones"), 1)
            for g in range(KVH):
                if g >= 2:
                    pool.wait_ge(sem("pv_done"), STEPS * (g - 1))
                pool.tensor_copy(VS[:, g % 2, :, 0:HD], V16[:, g]).then_inc(sem("vs_done"), 1)
            for tick in range(TT + 8):
                t = tick - 8
                if 0 <= t < TT:
                    pool.wait_ge(sem("zs_done"), t + 1)
                    pool.tensor_tensor(ZO[:, t % 2], ZO[:, t % 2], X[:, t], ALU.add).then_inc(sem("zo_done"), 1)
                t = tick - 3
                if 0 <= t < TT:
                    if t == 0:
                        pool.wait_ge(sem("tail_loaded"), 96)
                    pool.wait_ge(sem("xe_done"), t + 1)
                    pool.tensor_tensor(X[:, t], X[:, t], BIASF[:], ALU.add).then_inc(sem("biasf_done"), 1)
                t = tick - 2
                if 0 <= t < TT:
                    rstd(slice(t, t + 1), 2 + 2 * TT + t)

        @block.scalar
        def _(act):
            act.wait_ge(sem("w0m_done"), 1)
            act.activation(W0H[:], W0[:], ACT.Copy).then_inc(sem("w0h_done"), 1)

            def high(n):
                kind, t = order[n]
                act.wait_ge(sem("tr_done"), n + 1)
                if kind == 2:
                    act.wait_ge(sem("y0_done"), t + 1)
                act.activation(XNH[:, :, P * t:P * t + P],
                               PS[:, n % 2].rearrange("p (k t) -> p k t", k=KT), ACT.Copy).then_inc(sem("xnh_done"), 1)

            high(0)
            high(1)
            for t in range(TT):
                if t >= 1:
                    high(seq[(2, t - 1)])
                if t + 2 < TT:
                    high(seq[(1, t + 2)])
                if t < 6:
                    act.wait_ge(sem(f"raw_loaded{t % 2}"), 16 * (t // 2 + 1))
                    dst = SGQ[:, t] if t < 4 else SGKV[:, 2 * (t - 4):2 * (t - 4) + 2].rearrange("p k n -> p (k n)")
                    act.activation(dst, RAW[:, t % 2], ACT.Sign).then_inc(sem("sign_done"), 1)
                    if t >= 2:
                        act.wait_ge(sem("abs_used"), t - 1)
                    act.activation(ABS[:, t % 2], RAW[:, t % 2], ACT.Abs).then_inc(sem("abs_done"), 1)
            high(seq[(2, TT - 1)])

            def w_high(h, par, slot, first):
                act.wait_ge(sem("wf_done"), h + 1)
                if not first:
                    act.wait_ge(sem("up_done"), (h - 1) * 2)
                act.activation(WH[:, par], WF[:].rearrange("p (w k) o -> p w k o", w=2), ACT.Copy).then_inc(
                    sem("wh_done"), 1)
                act.wait_ge(sem("w2f_done"), h + 1)
                act.activation(W2H[:, slot], W2F[:], ACT.Copy).then_inc(sem("w2h_done"), 1)

            def hidden(n, h, c, pair, slot):
                act.wait_ge(sem("up_done"), n + 1)
                if n >= 2:
                    act.wait_ge(sem("u_done"), n - 1)
                act.activation(TH[:, c], PS[:, 2 * pair], ACT.Tanh, scale=0.5).then_inc(sem("th_done"), 1)
                act.wait_ge(sem("hf_done"), n + 1)
                act.activation(HH[:, slot, DIM * c:DIM * c + DIM], HF[:, c], ACT.Copy).then_inc(sem("hh_done"), 1)

            w_high(0, 0, 0, True)
            w_high(1, 1, 1, True)
            for half in range(2):
                h0, h1 = HALVES[half], HALVES[half + 1]
                for h in range(h0, h1):
                    if half and h == h0:
                        act.wait_ge(sem("down_done"), TT)
                        w_high(h, h % 2, 0, False)
                        w_high(h + 1, (h + 1) % 2, 1, False)
                    for c in range(CH):
                        hidden(2 * h + c, h, c, (2 * h + c) % 4, h - h0)
                    if h + 2 < h1:
                        w_high(h + 2, h % 2, h + 2 - h0, False)
            for t in range(TT):
                act.wait_ge(sem("tr3_done"), t + 1)
                act.activation(XNH[:, :, P * t:P * t + P],
                               PS[:, 2 + t % 2].rearrange("p (k t) -> p k t", k=KT), ACT.Copy).then_inc(sem("xnh3_done"), 1)
            for u in range(12):
                c, i = u // 6, u % 6
                cs = slice(DIM * c, DIM * c + DIM)
                act.wait_ge(sem("proj_done"), u + 1)
                if u >= 2:
                    act.wait_ge(sem("finite_done"), u - 1)
                if i == 1:
                    act.activation(YS[:, u % 2], PS[:, 4 + u % 4], ACT.Copy).then_inc(sem("ys_done"), 1)
                else:
                    col = 4 if i == 0 else i - 2
                    act.activation(YS[:, u % 2], PS[:, 4 + u % 4], ACT.Copy, scale=SQK[:, col:col + 1]).then_inc(
                        sem("ys_done"), 1)
                act.wait_ge(sem("finite_done"), u + 1)
                if i == 1:
                    act.sem_inc(sem("part_hi"), 1)
                    act.sem_inc(sem("part_mid"), 1)
                    act.wait_ge(sem("split_done"), u + 1)
                    act.sem_inc(sem("rest_done"), 1)
                    continue
                parts = KP if i == 0 else QP[:, i - 2]
                act.activation(parts[:, 0, cs], YP[:], ACT.Copy).then_inc(sem("part_hi"), 1)
                act.wait_ge(sem("rest_done"), u + 1)
                act.activation(parts[:, 1, cs], YN[:], ACT.Copy).then_inc(sem("part_mid"), 1)

            def maxima(g):
                act.wait_ge(sem("nmt_done"), g + 1)
                act.activation(MT[:, g % 2], PS[0:3 * MAXT, 7, 0:P // 2].bitcast(BF16), ACT.Copy).then_inc(
                    sem("mt_done"), 1)

            maxima(0)
            for g in range(KVH):
                for s in range(STEPS):
                    S = STEPS * g + s
                    for j in range(REP):
                        n = REP * S + j
                        act.wait_ge(sem("keyscore_done"), n + 1)
                        if j == 0 and S >= 2:
                            act.wait_ge(sem("pv_done"), S - 1)
                        act.activation(PR[:, S % 2, j], PS[:, n % 2], ACT.Exp, scale=float(HD) ** -0.5).then_inc(
                            sem("exp_done"), 1)
                    if s == 14 and g + 1 < KVH:
                        maxima(g + 1)
                    if s % TT == 0 and S > 0:
                        act.wait_ge(sem("pv_done"), S)
                        m = S // TT - 1
                        act.activation(OT[m % 2][:, m // 2], PS[:, 6], ACT.Copy).then_inc(sem("ot_done"), 1)
            act.wait_ge(sem("pv_done"), STEPS * KVH)
            act.activation(OT[1][:, KVH - 1], PS[:, 6], ACT.Copy).then_inc(sem("ot_done"), 1)
            act.wait_ge(sem("tail_loaded"), 96)
            act.activation(ABSO[:], RAWO[:], ACT.Abs).then_inc(sem("abso_done"), 1)
            act.activation(SGO[:], RAWO[:], ACT.Sign).then_inc(sem("sgo_done"), 1)
            act.activation(SGF[:], RAWF[:], ACT.Sign).then_inc(sem("sgf_done"), 1)
            act.wait_ge(sem("css_loaded"), 48)
            act.activation(CSS[:], CSA[:], ACT.Copy).then_inc(sem("css_done"), 1)

            def high_e(kind, t, bank):
                act.wait_ge(sem(f"te{kind}_done"), t + 1)
                if t >= 2:
                    act.wait_ge(sem(f"ue{kind}_done"), t - 1)
                act.activation(EH[:, kind, t % 2], PS[:, bank].rearrange("p (k t) -> p k t", k=KT),
                               ACT.Copy).then_inc(sem(f"he{kind}_done"), 1)

            for tick in range(TT + 8):
                t = tick - 7
                if 0 <= t < TT:
                    high_e(2, t, 4)
                t = tick - 6
                if 0 <= t < TT:
                    act.wait_ge(sem("cs_done"), t + 1)
                    if t >= 3:
                        act.wait_ge(sem("zs_done"), t - 2)
                    act.activation(OS[:, t % 3], PS[:, 7], ACT.Copy).then_inc(sem("os_done"), 1)
                t = tick - 5
                if 0 <= t < TT:
                    act.wait_ge(sem("rt_turned"), t + 1)
                    if t >= 1:
                        act.wait_ge(sem("cs_done"), t)
                    act.activation(RT[:], PS[0:3 * EXP, 5, P:2 * P], ACT.Copy).then_inc(sem("rt_done"), 1)
                t = tick - 4
                if 0 <= t < TT:
                    act.wait_ge(sem("lmax_done"), t + 1)
                    act.activation(RE[:], PS[:, 5, 0:EXP], ACT.Exp, bias=RM[:, 1:2],
                                   accum_out=RM[:, 2:3]).then_inc(sem("re_done"), 1)
                t = tick - 3
                if 0 <= t < TT:
                    high_e(1, t, 4)
                t = tick - 1
                if 0 <= t < TT:
                    high_e(0, t, 2)

        @block.vector
        def _(dve):
            dve.wait_ge(sem("w0_loaded"), 32)
            dve.tensor_reduce(BSUM[:], M0[:].rearrange("p k (b e) -> p (k b) e", e=32), AX, ALU.add).then_inc(
                sem("bsum_done"), 1)

            def stats(t):
                dve.bn_stats(ST[:, t], X[:, t]).then_inc(sem("st_done"), 1)

            dve.wait_ge(sem("x_loaded"), 16)
            for t in range(TT):
                stats(t)
            dve.wait_ge(sem("st_done"), TT)
            for t in range(TT):
                dve.bn_aggr(MV[:, t], ST[:, t]).then_inc(sem("ag_done"), 1)
            dve.wait_ge(sem("ag_done"), TT)
            dve.tensor_scalar(MV[:, :, 1], MV[:, :, 1], EPS, None, ALU.add).then_inc(sem("mv_done"), 1)
            dve.wait_ge(sem("block_sums"), 1)
            dve.tensor_scalar(BON[:], PS[:, 4, 0:KT * 16], 0.0, None, ALU.is_gt).then_inc(sem("bon_done"), 1)
            dve.wait_ge(sem("bon_done"), 1)
            w0b = W0[:].rearrange("p k (b e) -> p (k b) e", e=32)
            dve.tensor_tensor(w0b, w0b, BON[:].rearrange("p (b o) -> p b o", o=1).broadcast_to([P, KT * 16, 32]),
                              ALU.mult).then_inc(sem("w0m_done"), 1)

            def normalise(n, t, n_rstd):
                dve.wait_ge(sem("rstd_done"), n_rstd)
                if n >= 3:
                    dve.wait_ge(sem("tr_done"), n - 2)
                src = X[:, t].rearrange("p (C c h j) -> p C h c j", C=2, c=2, h=2)
                dst = XN[:, n % 3].rearrange("p (C h c j) -> p C h c j", C=2, c=2, h=2)
                for C in range(2):
                    ins = dve.tensor_scalar(dst[:, C], src[:, C], MV[:, t, 0:1], RSTD[:, t:t + 1],
                                            ALU.subtract, ALU.mult)
                    if C == 0:
                        ins.then_inc(sem("xn_half"), 1)
                    else:
                        ins.then_inc(sem("xn_done"), 1)

            def low(n):
                kind, t = order[n]
                dve.wait_ge(sem("xnh_done"), n + 1)
                dve.tensor_tensor(XNL[:, :, P * t:P * t + P], PS[:, n % 2].rearrange("p (k t) -> p k t", k=KT),
                                  f32(XNH[:, :, P * t:P * t + P]), ALU.subtract).then_inc(sem("xnl_done"), 1)

            def residual_stats(t, k):
                dve.wait_ge(sem("resid_done"), k + 1)
                dve.bn_stats(ST[:, t], X[:, t]).then_inc(sem("st_done"), 1)
                dve.wait_ge(sem("st_done"), TT + k + 1)
                dve.bn_aggr(MV[:, t], ST[:, t]).then_inc(sem("ag_done"), 1)
                dve.wait_ge(sem("ag_done"), TT + k + 1)
                dve.tensor_scalar(MV[:, t, 1:2], MV[:, t, 1:2], EPS, None, ALU.add).then_inc(sem("mv_done"), 1)

            dve.wait_ge(sem("consts_loaded"), 16 * 7)
            dve.tensor_copy(IDB[:], ID[:]).then_inc(sem("idb_done"), 1)
            normalise(0, 0, 1)
            normalise(1, 1, 1)
            low(0)
            low(1)
            for t in range(TT):
                if t + 2 < TT:
                    normalise(seq[(1, t + 2)], t + 2, 1)
                dve.wait_ge(sem("y0_done"), t + 1)
                dve.wait_ge(sem("bias_done"), t + 1)
                dve.tensor_tensor(X[:, t], PS[:, 2 + t % 2], X[:, t], ALU.add).then_inc(sem("resid_done"), 1)
                residual_stats(t, t)
                normalise(seq[(2, t)], t, 2 + t)
                if t >= 1:
                    low(seq[(2, t - 1)])
                if t + 2 < TT:
                    low(seq[(1, t + 2)])
            low(seq[(2, TT - 1)])
            dve.wait_ge(sem("abs_used"), 6)
            dve.tensor_scalar(SQK[:], PS[:, 5, 0:5], 1.0 / DIM, 1e-8, ALU.mult, ALU.max).then_inc(sem("sc_done"), 1)
            dve.tensor_scalar(SVB[:], PS[:, 6, 0:P], 1.0 / DIM, 1e-8, ALU.mult, ALU.max).then_inc(sem("sc_done"), 1)
            dve.wait_ge(sem("sc_done"), 2)
            dve.tensor_tensor(SQK[:], SQK[:], QKSC[:], ALU.mult).then_inc(sem("sc_done"), 1)
            dve.tensor_tensor(SVB[:], SVB[:], VSC[:], ALU.mult).then_inc(sem("sc_done"), 1)

            def unpack(h, par, first):
                dve.wait_ge(sem(f"p13_loaded{par}"), (h // 2 + 1) * 48)
                if not first:
                    dve.wait_ge(sem("wf_done"), h)
                dst = N13[:].rearrange("p (w b) o -> p w b o", b=2)
                dve.tensor_scalar(dst[:, :, 0], P13[:, par], 4, None, ALU.arith_shift_right).then_inc(
                    sem("n13_half"), 1)
                dve.tensor_scalar(dst[:, :, 1], P13[:, par], 28, 28, ALU.logical_shift_left,
                                  ALU.arith_shift_right).then_inc(sem("n13_done"), 1)
                dve.wait_ge(sem("n13_done"), h + 1)
                if not first:
                    dve.wait_ge(sem("wl_done"), h)
                    dve.wait_ge(sem("wh_done"), h)
                dve.tensor_tensor(WF[:], N13[:], S13[:, par], ALU.mult).then_inc(sem("wf_done"), 1)
                dve.wait_ge(sem(f"p2_loaded{par}"), (h // 2 + 1) * 80)
                if not first:
                    dve.wait_ge(sem("w2f_done"), h)
                for r in range(4):
                    ins = dve.tensor_scalar(N2[:].rearrange("p (v r) -> p r v", r=4)[:, r],
                                            P2[:, par].rearrange("p (v r) -> p r v", r=4)[:, r],
                                            SH2[:, r, 0:1], SH2[:, r, 1:2], ALU.logical_shift_left,
                                            ALU.arith_shift_right)
                    ins.then_inc(sem("n2_done") if r == 3 else sem("n2_part"), 1)
                dve.wait_ge(sem("n2_done"), h + 1)
                if not first:
                    dve.wait_ge(sem("w2l_done"), h)
                    dve.wait_ge(sem("w2h_done"), h)
                dve.tensor_tensor(W2F[:], N2[:], S2[:, par], ALU.mult).then_inc(sem("w2f_done"), 1)

            def gate(n, h, c, pair, slot):
                dve.wait_ge(sem("th_done"), n + 1)
                if n >= 2:
                    dve.wait_ge(sem("hf_done"), n - 1)
                dve.scalar_tensor_tensor(UU[:, c], TH[:, c], 1.0, PS[:, 2 * pair], ALU.add, ALU.mult).then_inc(
                    sem("u_done"), 1)
                dve.wait_ge(sem("u_done"), n + 1)
                if n >= 2:
                    dve.wait_ge(sem("hh_done"), n - 1)
                    dve.wait_ge(sem("hl_done"), n - 1)
                dve.scalar_tensor_tensor(HF[:, c], UU[:, c], 0.5, PS[:, 2 * pair + 1], ALU.mult, ALU.mult).then_inc(
                    sem("hf_done"), 1)
                dve.wait_ge(sem("hh_done"), n + 1)
                dve.tensor_tensor(HL[:, slot, DIM * c:DIM * c + DIM], HF[:, c],
                                  f32(HH[:, slot, DIM * c:DIM * c + DIM]), ALU.subtract).then_inc(sem("hl_done"), 1)

            def low3(t):
                dve.wait_ge(sem("xnh3_done"), t + 1)
                dve.tensor_tensor(XNL[:, :, P * t:P * t + P], PS[:, 2 + t % 2].rearrange("p (k t) -> p k t", k=KT),
                                  f32(XNH[:, :, P * t:P * t + P]), ALU.subtract).then_inc(sem("xnl3_done"), 1)

            unpack(0, 0, True)
            unpack(1, 1, False)
            for half in range(2):
                h0, h1 = HALVES[half], HALVES[half + 1]
                for h in range(h0, h1):
                    for c in range(CH):
                        gate(2 * h + c, h, c, (2 * h + c) % 4, h - h0)
                    if h + 2 < HT:
                        unpack(h + 2, h % 2, False)
                for t in range(TT):
                    k = TT * (half + 1) + t
                    dve.wait_ge(sem("down_done"), TT * half + t + 1)
                    bank = t if half == 0 else t % 2
                    dve.tensor_tensor(X[:, t], PS[:, bank], X[:, t], ALU.add).then_inc(sem("resid_done"), 1)
                    if half:
                        dve.wait_ge(sem("resid_done"), k + 1)
                        dve.bn_stats(ST[:, t], X[:, t]).then_inc(sem("st_done"), 1)
                        dve.wait_ge(sem("st_done"), 2 * TT + t + 1)
                        dve.bn_aggr(MV[:, t], ST[:, t]).then_inc(sem("ag_done"), 1)
                        dve.wait_ge(sem("ag_done"), 2 * TT + t + 1)
                        dve.tensor_scalar(MV[:, t, 1:2], MV[:, t, 1:2], EPS, None, ALU.add).then_inc(sem("mv_done"), 1)
                        dve.wait_ge(sem("rstd_done"), 2 + TT + t)
                        n = t
                        if n >= 3:
                            dve.wait_ge(sem("tr3_done"), n - 2)
                        src = X[:, t].rearrange("p (C c h j) -> p C h c j", C=2, c=2, h=2)
                        dst = XN[:, n % 3].rearrange("p (C h c j) -> p C h c j", C=2, c=2, h=2)
                        for C in range(2):
                            ins = dve.tensor_scalar(dst[:, C], src[:, C], MV[:, t, 0:1], RSTD[:, t:t + 1],
                                                    ALU.subtract, ALU.mult)
                            ins.then_inc(sem("xn3_done") if C else sem("xn3_half"), 1)
                        if t >= 1:
                            low3(t - 1)
            low3(TT - 1)

            def finite(y, pos, neg, fin, name, k):
                dve.tensor_scalar(pos, y, 0.0, 1e6, ALU.max, ALU.min).then_inc(sem(name + "_step"), 1)
                dve.tensor_scalar(neg, y, 0.0, -1e6, ALU.min, ALU.max).then_inc(sem(name + "_step"), 1)
                dve.tensor_scalar(fin, y, 0.0, 0.0, ALU.mult, ALU.is_equal).then_inc(sem(name + "_step"), 1)
                dve.wait_ge(sem(name + "_step"), 4 * k + 2)
                dve.tensor_tensor(pos, pos, neg, ALU.add).then_inc(sem(name + "_step"), 1)
                dve.wait_ge(sem(name + "_step"), 4 * k + 4)
                dve.copy_predicated(pos, fin.bitcast(I32), y).then_inc(sem(name + "_done"), 1)

            for u in range(12):
                dve.wait_ge(sem("ys_done"), u + 1)
                y = YS[:, u % 2]
                if u % 6 == 1:
                    y4 = y.rearrange("p (t o) -> p t o", t=4)
                    dve.tensor_tensor(y4, y4, SVB[:].rearrange("p (t o) -> p t o", t=1).broadcast_to([P, 4, P]),
                                      ALU.mult).then_inc(sem("v_scaled"), 1)
                    dve.wait_ge(sem("v_scaled"), u // 6 + 1)
                if u >= 1:
                    dve.wait_ge(sem("split_done"), u)
                finite(y, YP[:], YN[:], FIN[:], "finite", u)

            def row_max(g, i):
                dve.wait_ge(sem("score_done"), MAXT * g + i + 1)
                b = 2 + 2 * (i % 2)
                dve.tensor_reduce(MX[:, g % 2, i:i + 1], PS[:, b:b + 2], mybir.AxisListType.XY, ALU.max).then_inc(
                    sem("max_done"), 1)

            for g in range(KVH):
                for i in range(MAXT):
                    row_max(g, i)
                mx, nm = MX[:, g % 2], NM[:, g % 2]
                dve.wait_ge(sem("max_done"), MAXT * (g + 1))
                dve.tensor_scalar(nm[:, 0], mx, -1.0, None, ALU.mult).then_inc(sem("nm_step"), 1)
                dve.wait_ge(sem("nm_step"), 3 * g + 1)
                dve.scalar_tensor_tensor(MR[:], mx, -1.0, nm[:, 0], ALU.mult, ALU.subtract).then_inc(sem("nm_step"), 1)
                dve.wait_ge(sem("nm_step"), 3 * g + 2)
                dve.tensor_copy(nm[:, 1], MR[:]).then_inc(sem("nm_step"), 1)
                dve.wait_ge(sem("nm_step"), 3 * g + 3)
                dve.tensor_tensor(nm[:, 2], MR[:], nm[:, 1], ALU.subtract).then_inc(sem("nm_done"), 1)

            def normal_o(t):
                dve.wait_ge(sem("to_done"), t + 1)
                o = PS[:, 0:2].rearrange("p b (h c) -> p (b h) c", c=32)
                dve.reciprocal(DEN[:], o[:, :, HD]).then_inc(sem("den_done"), 1)
                dve.wait_ge(sem("den_done"), t + 1)
                if t >= 2:
                    dve.wait_ge(sem("te0_done"), t - 1)
                dve.tensor_tensor(ON[:, t % 2].rearrange("p (h c) -> p h c", c=HD), o[:, :, 0:HD],
                                  DEN[:].rearrange("p (h o) -> p h o", o=1).broadcast_to([P, HEADS, HD]),
                                  ALU.mult).then_inc(sem("on_done"), 1)

            dve.wait_ge(sem("tail_loaded"), 96)
            dve.tensor_copy(CSH[:], CS[:]).then_inc(sem("cs_split"), 1)
            dve.wait_ge(sem("cs_split"), 1)
            dve.tensor_tensor(CSL[:], CS[:], f32(CSH[:]), ALU.subtract).then_inc(sem("cs_split"), 1)
            dve.tensor_copy(GTH[:], GATE[:]).then_inc(sem("gate_split"), 1)
            dve.wait_ge(sem("gate_split"), 1)
            dve.tensor_tensor(GTL[:], GATE[:], f32(GTH[:]), ALU.subtract).then_inc(sem("gate_split"), 1)
            dve.wait_ge(sem("abso_sums"), 1)
            dve.tensor_scalar(SOB[:], PS[:, 3], 1.0 / DIM, 1e-8, ALU.mult, ALU.max).then_inc(sem("sob_done"), 1)
            dve.wait_ge(sem("sob_done"), 1)
            dve.tensor_tensor(SOB[:], SOB[:], OSC[:], ALU.mult).then_inc(sem("sob_done"), 1)

            def low_e(kind, t, bank):
                dve.wait_ge(sem(f"he{kind}_done"), t + 1)
                dve.tensor_tensor(EL[:, kind, t % 2], PS[:, bank].rearrange("p (k t) -> p k t", k=KT),
                                  f32(EH[:, kind, t % 2]), ALU.subtract).then_inc(sem(f"le{kind}_done"), 1)

            for tick in range(TT + 8):
                t = tick - 8
                if 0 <= t < TT:
                    dve.wait_ge(sem("ue2_done"), t + 1)
                    if t >= 2:
                        dve.wait_ge(sem(f"stored{t % 2}"), 16 * (t // 2))
                    dve.tensor_tensor(ZO[:, t % 2], PS[:, 3], OS[:, t % 3], ALU.mult).then_inc(sem("zs_done"), 1)
                t = tick - 7
                if 0 <= t < TT:
                    low_e(2, t, 4)
                t = tick - 6
                if 0 <= t < TT:
                    dve.wait_ge(sem("cs_done"), t + 1)
                    dve.tensor_tensor(ZI[:, t % 2], PS[:, 6], XE[:, t % 4], ALU.mult).then_inc(sem("zi_done"), 1)
                t = tick - 4
                if 0 <= t < TT:
                    dve.wait_ge(sem("ue1_done"), t + 1)
                    dve.tensor_reduce(RM[:, 0:1], PS[:, 5, 0:EXP], AX, ALU.max).then_inc(sem("lm_step"), 1)
                    dve.wait_ge(sem("lm_step"), t + 1)
                    dve.tensor_scalar(RM[:, 1:2], RM[:, 0:1], -1.0, None, ALU.mult).then_inc(sem("lmax_done"), 1)
                t = tick - 3
                if 0 <= t < TT:
                    dve.wait_ge(sem("rstd_done"), 2 + 2 * TT + t)
                    src = X[:, t].rearrange("p (C c h j) -> p C h c j", C=2, c=2, h=2)
                    dst = XE[:, t % 4].rearrange("p (C h c j) -> p C h c j", C=2, c=2, h=2)
                    for C in range(2):
                        dve.tensor_scalar(dst[:, C], src[:, C], MV[:, t, 0:1], RSTD[:, t:t + 1], ALU.subtract,
                                          ALU.mult).then_inc(sem("xe_done") if C else sem("xe_half"), 1)
                t = tick - 4
                if 0 <= t < TT:
                    dve.wait_ge(sem("re_done"), t + 1)
                    dve.reciprocal(RM[:, 3:4], RM[:, 2:3]).then_inc(sem("r_step"), 1)
                    dve.wait_ge(sem("r_step"), 3 * t + 1)
                    dve.tensor_scalar(RF[:], RE[:], RM[:, 3:4], None, ALU.mult).then_inc(sem("r_step"), 1)
                    dve.wait_ge(sem("r_step"), 3 * t + 2)
                    if t >= 1:
                        dve.wait_ge(sem("rt_turned"), t)
                    dve.tensor_copy(RH[:], RF[:]).then_inc(sem("r_step"), 1)
                    dve.wait_ge(sem("r_step"), 3 * t + 3)
                    dve.tensor_copy(RL[:, 0:EXP], f32(RH[:])).then_inc(sem("rl_part"), 1)
                    dve.tensor_copy(RL[:, 2 * EXP:], f32(RH[:])).then_inc(sem("rl_part"), 1)
                    dve.tensor_tensor(RL[:, EXP:2 * EXP], RF[:], f32(RH[:]), ALU.subtract).then_inc(sem("rl_done"), 1)
                t = tick - 2
                if 0 <= t < TT:
                    dve.wait_ge(sem("ue0_done"), t + 1)
                    dve.tensor_tensor(EYS[:], PS[:, 3], SOB[:], ALU.mult).then_inc(sem("eys_done"), 1)
                    dve.wait_ge(sem("eys_done"), t + 1)
                    finite(EYS[:], EYP[:], EYN[:], EFIN[:], "efinite", t)
                    dve.wait_ge(sem("efinite_done"), t + 1)
                    dve.tensor_tensor(X[:, t], X[:, t], EYP[:], ALU.add).then_inc(sem("resid4_done"), 1)
                    dve.wait_ge(sem("resid4_done"), t + 1)
                    dve.bn_stats(ST[:, t], X[:, t]).then_inc(sem("st_done"), 1)
                    dve.wait_ge(sem("st_done"), 3 * TT + t + 1)
                    dve.bn_aggr(MV[:, t], ST[:, t]).then_inc(sem("ag_done"), 1)
                    dve.wait_ge(sem("ag_done"), 3 * TT + t + 1)
                    dve.tensor_scalar(MV[:, t, 1:2], MV[:, t, 1:2], EPS, None, ALU.add).then_inc(sem("mv_done"), 1)
                t = tick - 3
                if 0 <= t < TT:
                    low_e(1, t, 4)
                t = tick
                if t < TT:
                    normal_o(t)
                t = tick - 1
                if 0 <= t < TT:
                    low_e(0, t, 2)

        @block.tensor
        def _(pe):
            pe.wait_ge(sem("consts_loaded"), 16 * 7)
            pe.wait_ge(sem("bsum_done"), 1)
            pe.matmul(PS[:, 4, 0:KT * 16], BLK[:], BSUM[:], start=True, stop=True).then_inc(sem("block_sums"), 1)

            def transpose(n):
                pe.wait_ge(sem("xn_done"), n + 1)
                if n >= 2:
                    pe.wait_ge(sem("xnl_done"), n - 1)
                for k in range(KT):
                    ins = pe.transpose(PS[:, n % 2, P * k:P * k + P], XN[:, n % 3, P * k:P * k + P], ID[:])
                ins.then_inc(sem("tr_done"), 1)

            def three(dst, stat, mov, first, last):
                pe.matmul(dst, stat[0], mov[0], start=first, stop=False)
                pe.matmul(dst, stat[0], mov[1], start=False, stop=False)
                return pe.matmul(dst, stat[1], mov[0], start=False, stop=last)

            transpose(0)
            transpose(1)
            for t in range(TT):
                pe.wait_ge(sem("xnl_done"), seq[(1, t)] + 1)
                if t == 0:
                    pe.wait_ge(sem("w0l_done"), 1)
                if t >= 2:
                    pe.wait_ge(sem("resid_done"), t - 1)
                ts = slice(P * t, P * t + P)
                for k in range(KT):
                    ins = three(PS[:, 2 + t % 2], (XNH[:, k, ts], XNL[:, k, ts]), (W0H[:, k], W0L[:, k]),
                                k == 0, k == KT - 1)
                ins.then_inc(sem("y0_done"), 1)
                if t >= 1:
                    transpose(seq[(2, t - 1)])
                if t + 2 < TT:
                    transpose(seq[(1, t + 2)])
                if 1 <= t < 7:
                    n = t - 1
                    pe.wait_ge(sem("abs_done"), n + 1)
                    a = ABS[:, n % 2]
                    if n < 4:
                        for T in range(4):
                            ins = pe.matmul(PS[:, 5, T:T + 1], a[:, P * T:P * T + P], ONES[:, 0:1],
                                            start=(n == 0 and T == 0), stop=(n == 3), skip_group_check=True)
                    else:
                        for kk in range(2):
                            b = a[:, 2 * P * kk:2 * P * kk + 2 * P]
                            pe.matmul(PS[:, 5, 4:5], b[:, 0:P], ONES[:, 0:1], start=False,
                                      stop=(n == 5 and kk == 1), skip_group_check=True)
                            ins = pe.matmul(PS[:, 6, 0:P], ONES[:], b[:, P:2 * P], start=(n == 4 and kk == 0),
                                            stop=(n == 5 and kk == 1))
                    ins.then_inc(sem("abs_used"), 1)
            transpose(seq[(2, TT - 1)])

            pe.wait_ge(sem("xnl_done"), NA)
            pe.wait_ge(sem("sc_done"), 4)
            for half in range(2):
                h0, h1 = HALVES[half], HALVES[half + 1]
                for h in range(h0, h1):
                    par = h % 2
                    pe.wait_ge(sem("wl_done"), h + 1)
                    for c in range(CH):
                        n = 2 * h + c
                        pair = n % 4
                        if n >= 4:
                            pe.wait_ge(sem("hf_done"), n - 3)
                        if half and n < 2 * h0 + 4:
                            pe.wait_ge(sem("resid_done"), TT + 2 * pair + 2)
                        cs = slice(DIM * c, DIM * c + DIM)
                        for w in range(2):
                            for k in range(KT):
                                ins = three(PS[:, 2 * pair + w], (WH[:, par, w, k], WL[:, par, w, k]),
                                            (XNH[:, k, cs], XNL[:, k, cs]), k == 0, k == KT - 1)
                        ins.then_inc(sem("up_done"), 1)
                pe.wait_ge(sem("hl_done"), 2 * h1)
                pe.wait_ge(sem("w2l_done"), h1)
                for t in range(TT):
                    ts = slice(P * t, P * t + P)
                    bank = t if half == 0 else t % 2
                    if half and t >= 2:
                        pe.wait_ge(sem("resid_done"), 2 * TT + t - 1)
                    for s in range(h1 - h0):
                        ins = three(PS[:, bank], (HH[:, s, ts], HL[:, s, ts]), (W2H[:, s], W2L[:, s]),
                                    s == 0, s == h1 - h0 - 1)
                    ins.then_inc(sem("down_done"), 1)
                    if half and t >= 1:
                        transpose3(pe, t - 1)
                if half:
                    def project(c, some):
                        for i in some:
                            u = 6 * c + i
                            bank = 4 + u % 4
                            if u >= 4:
                                pe.wait_ge(sem("ys_done"), u - 3)
                            cs = slice(DIM * c, DIM * c + DIM)
                            if i == 1:
                                for tt in range(4):
                                    ts = slice(DIM * c + P * tt, DIM * c + P * tt + P)
                                    for k in range(KT):
                                        for x in (XNH, XNL):
                                            ins = pe.matmul(PS[:, bank, P * tt:P * tt + P], x[:, k, ts],
                                                            SGKV[:, k, P:2 * P], start=(k == 0 and x is XNH),
                                                            stop=(k == KT - 1 and x is XNL))
                            else:
                                for k in range(KT):
                                    w = SGKV[:, k, 0:P] if i == 0 else SGQ[:, k, P * (i - 2):P * (i - 2) + P]
                                    for x in (XNH, XNL):
                                        ins = pe.matmul(PS[:, bank], w, x[:, k, cs], start=(k == 0 and x is XNH),
                                                        stop=(k == KT - 1 and x is XNL))
                            ins.then_inc(sem("proj_done"), 1)

                    pe.wait_ge(sem("xnl3_done"), 4)
                    project(0, range(4))
                    transpose3(pe, TT - 1)
                    project(0, range(4, 6))
                    pe.wait_ge(sem("xnl3_done"), TT)
                    project(1, range(6))

            def score_rows(g, i):
                b = 2 + 2 * (i % 2)
                n = MAXT * g + i
                if n >= 2:
                    pe.wait_ge(sem("max_done"), n - 1)
                j, qt = i // TT, i % TT
                for c in range(CH):
                    ins = pe.matmul(PS[:, b + c], QS[0:SROWS, REP * g + j, P * qt:P * qt + P],
                                    KS[0:SROWS, g, DIM * c:DIM * c + DIM], start=True, stop=True)
                ins.then_inc(sem("score_done"), 1)

            def maxima(g):
                pe.wait_ge(sem("nm_done"), g + 1)
                pe.transpose(PS[0:3 * MAXT, 7, 0:P // 2].bitcast(BF16), NM[:, g % 2].rearrange("p a i -> p (a i)"),
                             IDB[:]).then_inc(sem("nmt_done"), 1)

            def score_cols(S, j):
                n = REP * S + j
                g, s = S // STEPS, S % STEPS
                c, kt = s // TT, s % TT
                if s == 0 and j == 0:
                    pe.wait_ge(sem("m_loaded"), 16 * (g + 1))
                if n >= 2:
                    pe.wait_ge(sem("exp_done"), n - 1)
                pe.matmul(PS[:, n % 2], KS[0:MROWS, g, P * kt:P * kt + P],
                          QS[0:MROWS, REP * g + j, DIM * c:DIM * c + DIM], start=True, stop=True).then_inc(
                    sem("keyscore_done"), 1)

            def weigh(S):
                g, s = S // STEPS, S % STEPS
                kt = s % TT
                pe.wait_ge(sem("exp_done"), REP * (S + 1))
                if s == 0:
                    pe.wait_ge(sem("vs_done"), g + 1)
                if kt == 0 and S > 0:
                    pe.wait_ge(sem("ot_done"), S // TT)
                for j in range(REP):
                    ins = pe.matmul(PS[32 * j:32 * j + 32, 6], VS[:, g % 2, kt], PR[:, S % 2, j], start=(kt == 0),
                                    stop=(kt == TT - 1), tile_position=(0, 32 * j))
                ins.then_inc(sem("pv_done"), 1)

            pe.wait_ge(sem("idb_done"), 1)
            pe.wait_ge(sem("ks_ones"), 1)
            pe.wait_ge(sem("ys_done"), 12)
            pe.wait_ge(sem("ks0_loaded"), 16 * NTERM)
            pe.wait_ge(sem("qs_loaded"), 16 * REP * NTERM)
            for i in range(MAXT):
                score_rows(0, i)
            maxima(0)
            for j in range(REP):
                score_cols(0, j)
            pe.wait_ge(sem("ks_loaded"), 16 * NTERM * (KVH - 1))
            for g in range(KVH):
                for s in range(STEPS):
                    S = STEPS * g + s
                    tiles = range(0)
                    if g + 1 < KVH and s < MAXSTEPS:
                        tiles = range(s * MAXT // MAXSTEPS, (s + 1) * MAXT // MAXSTEPS)
                        if s == 0:
                            pe.wait_ge(sem("qs_loaded"), 16 * REP * NTERM * (g + 2))
                    if g + 1 < KVH and s == MAXSTEPS:
                        maxima(g + 1)
                    for j in range(REP):
                        if S + 1 < KVH * STEPS:
                            score_cols(S + 1, j)
                        if j < len(tiles):
                            score_rows(g + 1, tiles[j])
                    weigh(S)

            def turn_o(t):
                if t == 0:
                    pe.wait_ge(sem("ot_done"), 2 * KVH)
                if t >= 1:
                    pe.wait_ge(sem("on_done"), t)
                src = OT[t // 4]
                for g in range(KVH):
                    ins = pe.transpose(PS[:, g // 4, P * (g % 4):P * (g % 4) + P],
                                       src[:, g, P * (t % 4):P * (t % 4) + P], ID[:])
                ins.then_inc(sem("to_done"), 1)

            pe.wait_ge(sem("abso_done"), 1)
            for k in range(KT):
                ins = pe.matmul(PS[:, 3], ONES[:], ABSO[:, k], start=(k == 0), stop=(k == KT - 1))
            ins.then_inc(sem("abso_sums"), 1)

            def turn(kind, t, src, bank):
                for k in range(KT):
                    ins = pe.transpose(PS[:, bank, P * k:P * k + P], src[:, P * k:P * k + P], ID[:])
                ins.then_inc(sem(f"te{kind}_done"), 1)

            def by_signs(kind, t, w, bank):
                pe.wait_ge(sem(f"le{kind}_done"), t + 1)
                for k in range(KT):
                    pe.matmul(PS[:, bank], EH[:, kind, t % 2, k], w[:, k], start=(k == 0), stop=False)
                    ins = pe.matmul(PS[:, bank], EL[:, kind, t % 2, k], w[:, k], start=False, stop=(k == KT - 1))
                ins.then_inc(sem(f"ue{kind}_done"), 1)

            for tick in range(TT + 8):
                t = tick - 8
                if 0 <= t < TT:
                    if t == 0:
                        pe.wait_ge(sem("sgf_done"), 1)
                    pe.wait_ge(sem("eys_done"), min(t + 6, TT))
                    by_signs(2, t, SGF, 3)
                t = tick - 7
                if 0 <= t < TT:
                    pe.wait_ge(sem("zi_done"), t + 1)
                    pe.wait_ge(sem("le1_done"), min(t + 4, TT))
                    turn(2, t, ZI[:, t % 2], 4)
                t = tick - 6
                if 0 <= t < TT:
                    pe.wait_ge(sem("rt_done"), t + 1)
                    if t == 0:
                        pe.wait_ge(sem("css_done"), 1)
                    else:
                        pe.wait_ge(sem("zi_done"), t)
                        pe.wait_ge(sem("os_done"), t)
                    pe.matmul(PS[:, 6], RT[:], CSS[:, 0:DIM], start=True, stop=True)
                    pe.matmul(PS[:, 7], RT[:], CSS[:, DIM:], start=True, stop=True).then_inc(sem("cs_done"), 1)
                t = tick - 5
                if 0 <= t < TT:
                    pe.wait_ge(sem("rl_done"), t + 1)
                    pe.transpose(PS[0:3 * EXP, 5, P:2 * P], RL[:], ID[:]).then_inc(sem("rt_turned"), 1)
                t = tick - 4
                if 0 <= t < TT:
                    pe.wait_ge(sem("le1_done"), t + 1)
                    if t == 0:
                        pe.wait_ge(sem("gate_split"), 2)
                    else:
                        pe.wait_ge(sem("rt_done"), t)
                    for k in range(KT):
                        ins = three(PS[:, 5, 0:EXP], (EH[:, 1, t % 2, k], EL[:, 1, t % 2, k]), (GTH[:, k], GTL[:, k]),
                                    k == 0, k == KT - 1)
                    ins.then_inc(sem("ue1_done"), 1)
                t = tick - 3
                if 0 <= t < TT:
                    pe.wait_ge(sem("xe_done"), t + 1)
                    if t >= 1:
                        pe.wait_ge(sem("le1_done"), t)
                    if t >= 4:
                        pe.wait_ge(sem("le2_done"), t - 3)
                    turn(1, t, XE[:, t % 4], 4)
                t = tick - 2
                if 0 <= t < TT:
                    if t == 0:
                        pe.wait_ge(sem("sgo_done"), 1)
                        pe.wait_ge(sem("sob_done"), 1)
                    if t >= 6:
                        pe.wait_ge(sem("zs_done"), t - 5)
                    by_signs(0, t, SGO, 3)
                t = tick - 1
                if 0 <= t < TT:
                    pe.wait_ge(sem("on_done"), t + 1)
                    if t >= 1:
                        pe.wait_ge(sem("le0_done"), t)
                    turn(0, t, ON[:, t % 2], 2)
                t = tick
                if t < TT:
                    turn_o(t)


def layout(inp):
    import numpy as np
    g = {k: np.ascontiguousarray(v) for k, v in inp.items()}

    def contraction(wT):
        n = wT.shape[1]
        return wT.reshape(2, 2, 2, 64, n).transpose(1, 3, 0, 2, 4).reshape(P, KT, n)

    def rows(a):
        return a.reshape(1, -1)

    pad = HT * P - HID

    def packed(w):
        w = np.concatenate([w.reshape(HID, 2, 2, 64), np.zeros((pad, 2, 2, 64), w.dtype)])
        return w.reshape(HT, P, 2, 2, 64).transpose(0, 3, 4, 2, 1).reshape(HT, P, 2, P)

    def scales(s):
        s = np.concatenate([s.reshape(HID, 2, 2, 2), np.zeros((pad, 2, 2, 2), s.dtype)])
        return s.reshape(HT, P, 2, 2, 2).transpose(0, 3, 2, 4, 1).reshape(HT, 2, 4, P)

    flat = np.arange(DIM * HID).reshape(DIM, HID)
    w2 = g["L0_ffn_w2"][flat // 128, flat % 64].T
    w2 = np.concatenate([w2, np.zeros((pad, DIM), w2.dtype)]).reshape(HT, P, DIM)
    s2 = g["L0_ffn_s2"][flat[:, ::32] // 64].T
    s2 = np.concatenate([s2, np.zeros((pad // 32, DIM), s2.dtype)]).reshape(HT, 4, DIM)
    half2 = (96 * np.arange(4)[None] + np.arange(P)[:, None]) % 128 // 64
    wq = contraction(g["L1_attn_q_weight"].T)
    wkv = contraction(np.concatenate([g["L1_attn_k_weight"], g["L1_attn_v_weight"]]).T)
    qkv = np.concatenate([wq.transpose(1, 0, 2), wkv.reshape(P, 2, DIM).transpose(1, 0, 2)])
    return {
        "x": g["L0_attn_data"].reshape(TT, P, DIM).transpose(1, 0, 2),
        "m0": contraction(g["L0_attn_mask"].T),
        "w0": contraction(g["L0_attn_weight"].T),
        "bias0": rows(g["L0_attn_bias"]),
        "p13": np.concatenate([packed(g["L0_ffn_w1"]), packed(g["L0_ffn_w3"])], axis=2),
        "s13": np.concatenate([scales(g["L0_ffn_s1"]), scales(g["L0_ffn_s3"])], axis=2),
        "p2": w2,
        "s2": s2,
        "sh2": np.stack([28 * half2, 4 + 24 * half2], axis=2).astype(np.int32),
        "wqkv": qkv,
        "qksc": np.concatenate([g["L1_attn_q_scale"].reshape(4, P), g["L1_attn_k_scale"].reshape(1, P)]).T,
        "vsc": rows(g["L1_attn_v_scale"]),
        "wo": g["L1_attn_o_weight"].T.reshape(KT, P, DIM).transpose(1, 0, 2),
        "osc": rows(g["L1_attn_o_scale"]),
        "wf": contraction(g["L1_ffn_weight"].T),
        "biasf": rows(g["L1_ffn_bias"]),
        "gate": contraction(g["L1_ffn_gate_w"].T),
        "cs": np.concatenate([g["L1_ffn_in_channel_scale"].reshape(EXP, 2, 2, 2, 64).transpose(0, 1, 3, 2, 4)
                              .reshape(EXP, DIM), g["L1_ffn_out_channel_scale"]], axis=1),
        "ident": np.eye(P, dtype=np.float32),
        "ones": np.ones((P, P), np.float32),
        "blk": np.kron(np.eye(4), np.ones((32, 32))).astype(np.float32),
    }


def kernel(**inputs):
    import numpy as np
    from concourse import bacc
    from concourse.bass_utils import run_bass_kernel_spmd

    arrays = {f"in_{k}": np.ascontiguousarray(v) for k, v in layout(inputs).items()}
    nc = bacc.Bacc("TRN2", target_bir_lowering=False, num_devices=1)
    A = {k[3:]: nc.dram_tensor(k, v.shape, mybir.dt.from_np(v.dtype), kind="ExternalInput").ap()
         for k, v in arrays.items()}
    out = nc.dram_tensor("out", (P, TT, DIM), F32, kind="ExternalOutput").ap()
    build(nc, A, out)
    r = run_bass_kernel_spmd(nc, [arrays], core_ids=[0])
    return r.results[0]["out"].transpose(1, 0, 2).reshape(1, TOK, DIM)
```

```python
from contextlib import ExitStack

import concourse.bass as bass
from concourse import mybir

F32 = mybir.dt.float32
F32R = mybir.dt.float32r
BF16 = mybir.dt.bfloat16
I32 = mybir.dt.int32
ALU = mybir.AluOpType
ACT = mybir.ActivationFunctionType
AX = mybir.AxisListType.X

P = 128
TOK, DIM, HID = 1024, 512, 1376
TT = TOK // P
KT = DIM // P
HT = -(-HID // P)
HALVES = (0, 6, HT)
CH = 2
HEADS, KVH, HD = 32, 8, 16
REP = HEADS // KVH
EXP = 8
EPS = 1e-5
NTERM = 6
Q_PART = (0, 0, 0, 1, 1, 2)
K_PART = (0, 1, 2, 0, 1, 0)
SROWS = NTERM * HD
MROWS = SROWS + 3
FULL = 3.4028235e38
UNITS = CH * KVH
PAIRS = UNITS // 2
QT = DIM // P
MAXT = REP * QT
KEYBANK = (0, 1, 7, 1)
BEHIND = (3, 1, 3, 1)
AHEAD = 8
CHAIN = (MAXT - AHEAD) // 2 + 1
RING = 4


def build(nc, A, out):
    with ExitStack() as ctx:
        sems = {}

        def sem(name):
            if name not in sems:
                sems[name] = ctx.enter_context(nc.semaphore(name))
            return sems[name]

        base = (nc.sbuf_base + 63) // 64 * 64
        size = {F32: 4, F32R: 4, BF16: 2, I32: 4}
        end = nc.sbuf_usable_end

        class Region:
            def __init__(self, start):
                self.at = start

            def __call__(self, name, shape, dt):
                n = size[dt]
                for s in shape[1:]:
                    n *= s
                t = nc.alloc_sbuf_tensor_at("sb_" + name, list(shape), dt, offset=self.at)
                self.at += -(-n // 32) * 32
                assert self.at <= end, (name, self.at, end)
                return t

        keep = Region(base)
        X = keep("X", [P, TT, DIM], F32)
        ID = keep("ID", [P, P], F32)
        IDB = keep("IDB", [P, P], BF16)
        ONES = keep("ONES", [P, P], F32)
        BLK = keep("BLK", [P, P], F32)
        ST = keep("ST", [P, TT, 6], F32)
        MV = keep("MV", [P, TT, 2], F32)
        RSTD = keep("RSTD", [P, TT], F32)
        NHALF = keep("NHALF", [P, TT], F32)
        SQK = keep("SQK", [P, 5], F32)
        QKSC = keep("QKSC", [P, 5], F32)
        SVB = keep("SVB", [P, P], F32)
        VSC = keep("VSC", [P, P], F32)
        BIAS0 = keep("BIAS0", [P, DIM], F32)
        SH2 = keep("SH2", [P, 4, 2], I32)
        xnh_at = keep.at
        XNH = keep("XNH", [P, KT, TOK], F32R)
        xnl_at = keep.at
        XNL = keep("XNL", [P, KT, TOK], F32R)
        xn_at = keep.at
        XN = keep("XN", [P, 3, DIM], F32)
        SGQ = keep("SGQ", [P, KT, DIM], F32R)
        SGKV = keep("SGKV", [P, KT, 2 * P], F32R)
        arena = keep.at
        ra = Region(arena)
        W0 = ra("W0", [P, KT, DIM], F32)
        M0 = ra("M0", [P, KT, DIM], I32)
        W0H = ra("W0H", [P, KT, DIM], F32R)
        W0L = ra("W0L", [P, KT, DIM], F32R)
        RAW = ra("RAW", [P, 2, DIM], F32)
        ABS = ra("ABS", [P, 2, DIM], F32)
        BSUM = ra("BSUM", [P, KT * 16], F32)
        BON = ra("BON", [P, KT * 16], F32)
        rf = Region(arena)
        HH = rf("HH", [P, HALVES[1], TOK], F32R)
        HL = rf("HL", [P, HALVES[1], TOK], F32R)
        W2H = rf("W2H", [P, HALVES[1], DIM], F32R)
        W2L = rf("W2L", [P, HALVES[1], DIM], F32R)
        WH = rf("WH", [P, 2, 2, KT, P], F32R)
        WL = rf("WL", [P, 2, 2, KT, P], F32R)
        P13 = rf("P13", [P, 2, 4, P], I32)
        S13 = rf("S13", [P, 2, 8, P], F32)
        N13 = rf("N13", [P, 8, P], I32)
        WF = rf("WF", [P, 8, P], F32)
        P2 = rf("P2", [P, 2, DIM], I32)
        S2 = rf("S2", [P, 2, DIM], F32)
        N2 = rf("N2", [P, DIM], I32)
        W2F = rf("W2F", [P, DIM], F32)
        TH = rf("TH", [P, 2, DIM], F32)
        UU = rf("UU", [P, 2, DIM], F32)
        HF = rf("HF", [P, 2, DIM], F32)
        rt = Region(arena)
        QS = rt("QS", [P, RING, REP, DIM], BF16)
        KS = rt("KS", [P, KVH, TOK], BF16)
        V16 = rt("V16", [P, KVH, TT, HD], F32)
        VS = rt("VS", [P, 2, TT, 32], F32)
        MX = rt("MX", [P, 2, MAXT], F32)
        MR = rt("MR", [P, MAXT], F32)
        NM = rt("NM", [P, 2, 3, MAXT], BF16)
        MT = rt("MT", [3 * MAXT, 2, P], BF16)
        free = rt.at
        QP = rt("QP", [P, 3, DIM], BF16)
        KP = rt("KP", [P, CH, 3, DIM], BF16)
        Y = rt("Y", [P, CH * 6, DIM], F32)
        YP = rt("YP", [P, 2, DIM], F32)
        YN = rt("YN", [P, 2, DIM], F32)
        FIN = rt("FIN", [P, DIM], F32)
        YC = Y[:, 0]
        late = rt.at
        rp = Region(xnh_at)
        PR = rp("PR", [P, 2, REP, DIM], F32)
        OT = rp("OT", [P, UNITS, DIM], F32)
        assert rp.at <= arena
        rl = Region(late)
        SGO = rl("SGO", [P, KT, DIM], F32R)
        SGF = rl("SGF", [P, KT, DIM], F32R)
        rawo_at = rl.at
        RAWO = rl("RAWO", [P, KT, DIM], F32)
        RAWF = rl("RAWF", [P, KT, DIM], F32)
        raw_end = rl.at
        SOB = rl("SOB", [P, DIM], F32)
        OSC = rl("OSC", [P, DIM], F32)
        BIASF = rl("BIASF", [P, DIM], F32)
        GATE = rl("GATE", [P, KT, EXP], F32)
        GTH = rl("GTH", [P, KT, EXP], F32R)
        GTL = rl("GTL", [P, KT, EXP], F32R)
        CS = rl("CS", [EXP, 2 * DIM], F32)
        CSH = rl("CSH", [EXP, 2 * DIM], F32R)
        CSA = rl("CSA", [3 * EXP, 2 * DIM], F32)
        CSS = rl("CSS", [3 * EXP, 2 * DIM], F32R)
        re = Region(free)
        ON = re("ON", [P, 2, DIM], F32)
        XE = re("XE", [P, 4, DIM], F32)
        EH = re("EH", [P, 3, 2, KT, P], F32R)
        EL = re("EL", [P, 3, 2, KT, P], F32R)
        DEN = re("DEN", [P, HEADS], F32)
        RM = re("RM", [P, 4], F32)
        RE = re("RE", [P, EXP], F32)
        RF = re("RF", [P, EXP], F32)
        RH = re("RH", [P, EXP], F32R)
        RL = re("RL", [P, 3 * EXP], F32)
        RT = re("RT", [3 * EXP, P], F32R)
        assert re.at <= late
        ra = Region(arena)
        ZI = ra("ZI", [P, 2, DIM], F32)
        OS = ra("OS", [P, 3, DIM], F32)
        ZO = ra("ZO", [P, 2, DIM], F32)
        assert ra.at <= free
        rb = Region(rawo_at)
        EF = rb("EF", [P, 2, 2, KT, P], F32)
        EYS = rb("EYS", [P, DIM], F32)
        EYP = rb("EYP", [P, DIM], F32)
        EYN = rb("EYN", [P, DIM], F32)
        EFIN = rb("EFIN", [P, DIM], F32)
        assert rb.at <= raw_end

        PS = ctx.enter_context(nc.psum_tensor("PS", [P, 8, DIM], F32))

        f32 = lambda ap: ap.bitcast(F32)

        order = [(1, 0), (1, 1)]
        for t in range(TT):
            if t >= 1:
                order.append((2, t - 1))
            if t + 2 < TT:
                order.append((1, t + 2))
        order.append((2, TT - 1))
        seq = {k: n for n, k in enumerate(order)}
        NA = len(order)
        block = ctx.enter_context(nc.Block())

        def half_of(h):
            return 0 if h < HALVES[1] else 1

        PROJ = [("k", 0, 0), ("q", 0, 0), ("v", 0, 0)] + [("q", 0, T) for T in range(1, 4)] + [("k", 1, 0), ("v", 1, 0)] + [
            ("q", 1, T) for T in range(4)]
        PBANK = (6, 7, 0, 1)
        EARLY = (("k", 0), ("q", 0), ("v", 0), ("k", 1), ("v", 1))
        YQ = 4
        TICK_AT = ((UNITS - 2, 6), (UNITS - 1, 1), (UNITS - 1, 4))
        EARLY_TICKS = len(TICK_AT)

        def slot_of(proj):
            kind, c, T = proj
            return {"k": c, "v": 2 + c, "q": YQ + 4 * c + T}[kind]

        def transpose3(pe, t):
            pe.wait_ge(sem("xn3_done"), t + 1)
            if t >= 2:
                pe.wait_ge(sem("xnl3_done"), t - 1)
            for k in range(KT):
                ins = pe.transpose(PS[:, 2 + t % 2, P * k:P * k + P], XN[:, t % 3, P * k:P * k + P], ID[:])
            ins.then_inc(sem("tr3_done"), 1)

        @block.sync
        def _(sp):
            sp.dma_start(M0[:], A["m0"]).then_inc(sem("m0_loaded"), 16)
            sp.dma_start(X[:, 0:2], A["x"][:, 0:2]).then_inc(sem("x_loaded0"), 16)
            sp.dma_start(BLK[:], A["blk"]).then_inc(sem("blk_loaded"), 16)
            sp.dma_start(ID[:], A["ident"]).then_inc(sem("id_loaded"), 16)
            sp.dma_start(W0[:], A["w0"]).then_inc(sem("w0_loaded"), 16)
            for q in range(1, TT // 2):
                sp.dma_start(X[:, 2 * q:2 * q + 2], A["x"][:, 2 * q:2 * q + 2]).then_inc(sem(f"x_loaded{q}"), 16)
            for dst, src in ((BIAS0[:], "bias0"), (ONES[:], "ones"),
                             (SH2[:], "sh2"), (QKSC[:], "qksc"),
                             (VSC[:], "vsc")):
                ap = A[src]
                if src in ("bias0", "vsc"):
                    ap = ap.broadcast_to([P, ap.shape[1]])
                sp.dma_start(dst, ap).then_inc(sem("consts_loaded"), 16)

            def load_hidden(h, par, first):
                if not first:
                    sp.wait_ge(sem("n13_done"), h - 1)
                    sp.wait_ge(sem("wf_done"), h - 1)
                sp.dma_start(P13[:, par], A["p13"][h]).then_inc(sem(f"p13_loaded{par}"), 16)
                for c in range(2):
                    sp.dma_start(S13[64 * c:64 * c + 64, par],
                                 A["s13"][h, c:c + 1].broadcast_to([64, 8, P])).then_inc(sem(f"p13_loaded{par}"), 16)
                if not first:
                    sp.wait_ge(sem("n2_done"), h - 1)
                    sp.wait_ge(sem("w2f_done"), h - 1)
                sp.dma_start(P2[:, par], A["p2"][h]).then_inc(sem(f"p2_loaded{par}"), 16)
                for b in range(4):
                    sp.dma_start(S2[32 * b:32 * b + 32, par],
                                 A["s2"][h, b:b + 1].broadcast_to([32, DIM])).then_inc(sem(f"p2_loaded{par}"), 16)

            for n in range(6):
                if n >= 2:
                    sp.wait_ge(sem("abs_done"), n - 1)
                sp.dma_start(RAW[:, n % 2], A["wqkv"][n]).then_inc(sem(f"raw_loaded{n % 2}"), 16)
                if n == 1:
                    load_hidden(0, 0, True)
                    load_hidden(1, 1, True)
            with sp.Fori(1, HT // 2) as i:
                for par in range(2):
                    load_hidden(i * 2 + par, par, False)
            load_hidden(HT - 1, (HT - 1) % 2, False)
            def load_ks(c, parts=(0, 1, 2)):
                for r in (r for r in range(NTERM) if K_PART[r] in parts):
                    sp.dma_start(KS[HD * r:HD * r + HD, :, DIM * c:DIM * c + DIM], KP[:, c, K_PART[r]]).then_inc(
                        sem("ks_loaded"), 16)

            def load_qs(slot, par):
                for r in range(NTERM):
                    sp.dma_start(QS[HD * r:HD * r + HD, slot], QP[64 * par:64 * par + 64, Q_PART[r]]).then_inc(
                        sem("qs_loaded"), 16)

            def ahead(U, pair, slot, load):
                par = slot % 2
                if load:
                    if par == 0:
                        sp.wait_ge(sem("qp_done"), pair + 2)
                    else:
                        sp.wait_ge(sem("qs_loaded"), U * (16 * NTERM) + 32 * NTERM)
                    load_qs((slot + 2) % RING, par)
                sp.wait_ge(sem("mt_done"), U + 2)
                sp.dma_start(QS[SROWS:MROWS, (slot + 1) % RING].rearrange("p h (q c) -> p (h q) c", c=P),
                             MT[:, 1 - par]).then_inc(sem("m_loaded"), 16)

            sp.wait_ge(sem("kp_done"), 1)
            load_ks(0)
            sp.wait_ge(sem("qp_done"), 1)
            load_qs(0, 0)
            k1 = EARLY.index(("k", 1)) + 1
            for part, done in enumerate(("part_hi", "part_mid", "kp_done")):
                sp.wait_ge(sem(done), 2 if done == "kp_done" else k1)
                load_ks(1, (part,))
            sp.wait_ge(sem("qs_loaded"), 16 * NTERM)
            load_qs(1, 1)
            for dst, src in ((RAWO[:], A["wo"]), (RAWF[:], A["wf"]), (OSC[:], A["osc"].broadcast_to([P, DIM])),
                             (BIASF[:], A["biasf"].broadcast_to([P, DIM])), (GATE[:], A["gate"]),
                             (CS[:], A["cs"])):
                sp.dma_start(dst, src).then_inc(sem("tail_loaded"), 16)
            sp.wait_ge(sem("mt_done"), 1)
            sp.dma_start(QS[SROWS:MROWS, 0].rearrange("p h (q c) -> p (h q) c", c=P), MT[:, 0]).then_inc(
                sem("m_loaded"), 16)
            ahead(0, 0, 0, True)
            ahead(1, 0, 1, True)
            sp.wait_ge(sem("cs_split"), 2)
            for e, src in enumerate((f32(CSH[:]), f32(CSH[:]), CS[:])):
                sp.dma_start(CSA[EXP * e:EXP * e + EXP], src).then_inc(sem("css_loaded"), 16)
            with sp.Fori(0, (PAIRS - 2) // 2) as i:
                for k in range(RING):
                    ahead(i * RING + 2 + k, i * 2 + 1 + k // 2, (k + 2) % RING, True)
            ahead(UNITS - 2, PAIRS - 1, (UNITS - 2) % RING, False)
            for t in range(TT):
                sp.wait_ge(sem("zo_done"), t + 1)
                sp.dma_start(out[:, t], ZO[:, t % 2]).then_inc(sem(f"stored{t % 2}"), 16)
            for par in range(2):
                sp.wait_ge(sem(f"stored{par}"), 16 * (TT // 2))

        @block.gpsimd
        def _(pool):
            pool.memset(NHALF[:], -0.5).then_inc(sem("nhalf_done"), 1)
            pool.wait_ge(sem("nhalf_done"), 1)

            def rstd(sl, n_mv):
                pool.wait_ge(sem("mv_done"), n_mv)
                pool.tensor_tensor(RSTD[:, sl], MV[:, sl, 1], NHALF[:, sl], ALU.pow).then_inc(sem("rstd_done"), 1)

            rstd(slice(0, 2), 1)
            for k in range(KT):
                pool.wait_ge(sem("w0h_done"), k + 1)
                pool.tensor_tensor(W0L[:, k], W0[:, k], f32(W0H[:, k]), ALU.subtract).then_inc(sem("w0l_done"), 1)
            rstd(slice(2, TT), 2)
            pool.wait_ge(sem("consts_loaded"), 16 * 5)
            def low13(h, par):
                pool.wait_ge(sem("wh_done"), h + 1)
                pool.tensor_tensor(WL[:, par], WF[:].rearrange("p (w k) o -> p w k o", w=2), f32(WH[:, par]),
                                   ALU.subtract).then_inc(sem("wl_done"), 1)

            def low2(h, slot):
                pool.wait_ge(sem("w2h_done"), h + 1)
                pool.tensor_tensor(W2L[:, slot], W2F[:], f32(W2H[:, slot]), ALU.subtract).then_inc(sem("w2l_done"), 1)

            for t in range(TT):
                if t == TT - 1:
                    low13(0, 0)
                pool.wait_ge(sem("xn_done"), seq[(1, t)] + 1)
                pool.tensor_tensor(X[:, t], X[:, t], BIAS0[:], ALU.add).then_inc(sem("bias_done"), 1)
                rstd(slice(t, t + 1), 3 + t)

            low13(1, 1)
            for h in range(2):
                low2(h, h)
            for h in range(2, HT):
                low13(h, h % 2)
                low2(h, h - HALVES[half_of(h)])
            for t in range(TT):
                rstd(slice(t, t + 1), 3 + TT + t)

            def rest(u, b, dst):
                pool.wait_ge(sem("part_hi"), u + 1)
                pool.tensor_tensor(YN[:, b], YP[:, b], dst[0], ALU.subtract).then_inc(sem("rest_done"), 1)
                pool.wait_ge(sem("part_mid"), u + 1)
                pool.tensor_tensor(dst[2], YN[:, b], dst[1], ALU.subtract).then_inc(sem("split_done"), 1)

            for u, (kind, c) in enumerate(EARLY):
                pool.wait_ge(sem("finite_done"), u + 1)
                if kind == "v":
                    pool.tensor_copy(V16[:, :, QT * c:QT * c + QT].rearrange("p g t d -> p t g d"),
                                     YP[:, u % 2].rearrange("p (t g d) -> p t g d", t=QT, g=KVH)).then_inc(sem("split_done"), 1)
                else:
                    rest(u, u % 2, [KP[:, c, e] if kind == "k" else QP[:, e] for e in range(3)])
                    pool.wait_ge(sem("split_done"), u + 1)
                    pool.sem_inc(sem("kp_done") if kind == "k" else sem("qp_done"), 1)

            pool.wait_ge(sem("split_done"), len(EARLY))
            pool.memset(VS[:], 1.0).then_inc(sem("vs_ones"), 1)
            pool.wait_ge(sem("vs_ones"), 1)

            def scaled_output():
                pool.wait_ge(sem("sob_means"), 1)
                pool.tensor_scalar(SOB[:], SOB[:], 1e-8, None, ALU.max).then_inc(sem("sob_done"), 1)
                pool.wait_ge(sem("sob_done"), 1)
                pool.tensor_tensor(SOB[:], SOB[:], OSC[:], ALU.mult).then_inc(sem("sob_done"), 1)
                pool.wait_ge(sem("tail_high"), 2)
                pool.tensor_tensor(CS[:], CS[:], f32(CSH[:]), ALU.subtract).then_inc(sem("cs_split"), 2)
                pool.tensor_tensor(GTL[:], GATE[:], f32(GTH[:]), ALU.subtract).then_inc(sem("gate_split"), 2)

            def group_v(U, g, par, first):
                if not first:
                    pool.wait_ge(sem("pv_done"), TT * (U - 1))
                pool.tensor_copy(VS[:, par, :, 0:HD], V16[:, g]).then_inc(sem("vs_done"), 1)

            def guard(y):
                pool.tensor_scalar(YP[:, 0], y, 0.0, 1e6, ALU.max, ALU.min).then_inc(sem("guard_step"), 1)
                pool.tensor_scalar(YN[:, 0], y, 0.0, -1e6, ALU.min, ALU.max).then_inc(sem("guard_step"), 1)

            def next_q(i):
                pool.tensor_copy(YC, Y[:, YQ + i]).then_inc(sem("yc_done"), 1)
                pool.wait_ge(sem("yc_done"), i)
                pool.sem_inc(sem("yc_ready"), 1)
                guard(YC)
                pool.wait_ge(sem("guard_step"), i * 2)
                pool.tensor_tensor(YP[:, 0], YP[:, 0], YN[:, 0], ALU.add).then_inc(sem("guarded"), 1)
                rest(i + (len(EARLY) - 1), 0, [QP[:, e] for e in range(3)])
                pool.wait_ge(sem("split_done"), i + len(EARLY))
                pool.sem_inc(sem("qp_done"), 1)

            group_v(0, 0, 0, True)
            next_q(1)
            pool.memset(KS[SROWS:MROWS], 1.0).then_inc(sem("ks_ones"), 1)
            pool.wait_ge(sem("ks_ones"), 1)
            group_v(1, 1, 1, True)
            scaled_output()
            with pool.Fori(1, PAIRS - 1) as i:
                group_v(i * 2, (i & 3) * 2, 0, False)
                next_q(i + 1)
                group_v(i * 2 + 1, (i & 3) * 2 + 1, 1, False)
            for par in range(2):
                group_v(UNITS - 2 + par, KVH - 2 + par, par, False)

            def low_e(kind, t):
                pool.wait_ge(sem(f"he{kind}_done"), t + 1)
                pool.tensor_tensor(EL[:, kind, t % 2], EF[:, kind, t % 2], f32(EH[:, kind, t % 2]),
                                   ALU.subtract).then_inc(sem(f"le{kind}_done"), 1)

            for tick in range(TT + 8):
                t = tick - 3
                if 0 <= t < TT:
                    low_e(1, t)
                t = tick - 2
                if 0 <= t < TT:
                    rstd(slice(t, t + 1), 3 + 2 * TT + t)
                t = tick - 1
                if 0 <= t < TT:
                    low_e(0, t)
                t = tick - 8
                if 0 <= t < TT:
                    pool.wait_ge(sem("zs_done"), t + 1)
                    pool.tensor_tensor(ZO[:, t % 2], ZO[:, t % 2], X[:, t], ALU.add).then_inc(sem("zo_done"), 1)
                t = tick - 3
                if 0 <= t < TT:
                    if t == 0:
                        pool.wait_ge(sem("tail_loaded"), 96)
                    pool.wait_ge(sem("xe_done"), t + 1)
                    pool.tensor_tensor(X[:, t], X[:, t], BIASF[:], ALU.add).then_inc(sem("biasf_done"), 1)

        @block.scalar
        def _(act):
            def weight_high(k):
                act.wait_ge(sem("w0m_done"), k + 1)
                act.activation(W0H[:, k], W0[:, k], ACT.Copy).then_inc(sem("w0h_done"), 1)

            def high(n):
                kind, t = order[n]
                act.wait_ge(sem("tr_done"), n + 1)
                if kind == 2:
                    act.wait_ge(sem("y0_done"), t + 1)
                act.activation(XNH[:, :, P * t:P * t + P],
                               PS[:, n % 2].rearrange("p (k t) -> p k t", k=KT), ACT.Copy).then_inc(sem("xnh_done"), 1)

            def w_high(h, par, first):
                act.wait_ge(sem("wf_done"), h + 1)
                if not first:
                    act.wait_ge(sem("up_done"), (h - 1) * 2)
                act.activation(WH[:, par], WF[:].rearrange("p (w k) o -> p w k o", w=2), ACT.Copy).then_inc(
                    sem("wh_done"), 1)

            high(0)
            high(1)
            for k in range(KT):
                weight_high(k)
            for t in range(TT):
                if t >= 1:
                    high(seq[(2, t - 1)])
                if t + 2 < TT:
                    high(seq[(1, t + 2)])
                if t < 6:
                    act.wait_ge(sem(f"raw_loaded{t % 2}"), 16 * (t // 2 + 1))
                    dst = SGQ[:, t] if t < 4 else SGKV[:, 2 * (t - 4):2 * (t - 4) + 2].rearrange("p k n -> p (k n)")
                    act.activation(dst, RAW[:, t % 2], ACT.Sign).then_inc(sem("sign_done"), 1)
                    if t >= 2:
                        act.wait_ge(sem("abs_used"), t - 1)
                    act.activation(ABS[:, t % 2], RAW[:, t % 2], ACT.Abs).then_inc(sem("abs_done"), 1)
                if t == TT - 2:
                    w_high(0, 0, True)
            w_high(1, 1, True)
            high(seq[(2, TT - 1)])

            def w2_high(h, slot):
                act.wait_ge(sem("w2f_done"), h + 1)
                act.activation(W2H[:, slot], W2F[:], ACT.Copy).then_inc(sem("w2h_done"), 1)

            def hidden(n, h, c, pair, slot):
                act.wait_ge(sem("up_done"), n + 1)
                if n >= 2:
                    act.wait_ge(sem("u_done"), n - 1)
                act.activation(TH[:, c], PS[:, 2 * pair], ACT.Tanh, scale=0.5).then_inc(sem("th_done"), 1)
                act.wait_ge(sem("hf_done"), n + 1)
                act.activation(HH[:, slot, DIM * c:DIM * c + DIM], HF[:, c], ACT.Copy).then_inc(sem("hh_done"), 1)

            for h in range(2):
                w2_high(h, h)
            for half in range(2):
                h0, h1 = HALVES[half], HALVES[half + 1]
                for h in range(h0, h1):
                    if half and h == h0:
                        act.wait_ge(sem("down_done"), TT)
                        w2_high(h, 0)
                        w_high(h + 1, (h + 1) % 2, False)
                        w2_high(h + 1, 1)
                    for c in range(CH):
                        hidden(2 * h + c, h, c, (2 * h + c + 3) % 4, h - h0)
                    if h + 2 < h1:
                        w_high(h + 2, h % 2, False)
                        w2_high(h + 2, h + 2 - h0)
                if half == 0:
                    w_high(h1, h1 % 2, False)
            for t in range(TT):
                act.wait_ge(sem("tr3_done"), t + 1)
                act.activation(XNH[:, :, P * t:P * t + P],
                               PS[:, 2 + t % 2].rearrange("p (k t) -> p k t", k=KT), ACT.Copy).then_inc(sem("xnh3_done"), 1)
            def take(u):
                kind, c, T = PROJ[u]
                act.wait_ge(sem("proj_done"), u + 1)
                if kind == "v":
                    act.activation(Y[:, slot_of(PROJ[u])], PS[:, PBANK[u % 4]], ACT.Copy).then_inc(sem("ys_done"), 1)
                else:
                    col = 4 if kind == "k" else T
                    act.activation(Y[:, slot_of(PROJ[u])], PS[:, PBANK[u % 4]], ACT.Copy,
                                   scale=SQK[:, col:col + 1]).then_inc(sem("ys_done"), 1)

            def high_part(b, dst):
                act.activation(dst, YP[:, b], ACT.Copy).then_inc(sem("part_hi"), 1)

            def middle_part(u, b, dst):
                act.wait_ge(sem("rest_done"), u + 1)
                act.activation(dst, YN[:, b], ACT.Copy).then_inc(sem("part_mid"), 1)

            taken = 0
            for u, (kind, c) in enumerate(EARLY):
                while taken < len(PROJ) and taken < (3, 4, 6, 8, 12)[u]:
                    take(taken)
                    taken += 1
                act.wait_ge(sem("finite_done"), u + 1)
                if kind == "v":
                    act.wait_ge(sem("split_done"), u + 1)
                    act.sem_inc(sem("part_hi"), 1)
                    act.sem_inc(sem("part_mid"), 1)
                    act.sem_inc(sem("rest_done"), 1)
                else:
                    high_part(u % 2, KP[:, c, 0] if kind == "k" else QP[:, 0])
                    middle_part(u, u % 2, KP[:, c, 1] if kind == "k" else QP[:, 1])

            act.wait_ge(sem("tail_loaded"), 16 * 6)
            act.activation(SGO[:], RAWO[:], ACT.Sign).then_inc(sem("sgo_done"), 1)
            act.wait_ge(sem("sgo_done"), 1)
            act.activation(RAWO[:], RAWO[:], ACT.Abs).then_inc(sem("abso_done"), 1)
            act.activation(SGF[:], RAWF[:], ACT.Sign).then_inc(sem("sgf_done"), 1)
            act.activation(CSH[:], CS[:], ACT.Copy).then_inc(sem("tail_high"), 1)
            act.activation(GTH[:], GATE[:], ACT.Copy).then_inc(sem("tail_high"), 1)

            def maxima(U, par):
                act.wait_ge(sem("nmt_done"), U + 1)
                act.activation(MT[:, par], PS[0:3 * MAXT, KEYBANK[2], 0:P // 2].bitcast(BF16), ACT.Copy).then_inc(
                    sem("mt_done"), 1)

            act.wait_ge(sem("qs_loaded"), 2 * 16 * NTERM)
            act.wait_ge(sem("finite_done"), 1 + len(EARLY))
            high_part(0, QP[:, 0])
            middle_part(len(EARLY), 0, QP[:, 1])
            maxima(0, 0)
            act.wait_ge(sem("abso_sums"), 1)
            act.activation(SOB[:], PS[:, 6], ACT.Copy, scale=1.0 / DIM).then_inc(sem("sob_means"), 1)

            def high_e(kind, t, bank):
                act.wait_ge(sem(f"te{kind}_done"), t + 1)
                if t >= 2:
                    act.wait_ge(sem(f"ue{kind}_done"), t - 1)
                if kind in [0, 1]:
                    act.activation(EF[:, kind, t % 2], PS[:, bank].rearrange("p (k t) -> p k t", k=KT),
                                   ACT.Copy).then_inc(sem("ef_done"), 1)
                act.activation(EH[:, kind, t % 2], PS[:, bank].rearrange("p (k t) -> p k t", k=KT),
                               ACT.Copy).then_inc(sem(f"he{kind}_done"), 1)

            def attend(U, par, first, last, q):
                for s in range(TT):
                    S = U * TT + s
                    for j in range(REP):
                        act.wait_ge(sem("keyscore_done"), S * REP + j + 1)
                        if j == 0 and not (first and s < 2):
                            act.wait_ge(sem("pv_done"), S - 1)
                        act.activation(PR[:, s % 2, j], PS[:, KEYBANK[j]], ACT.Exp, scale=float(HD) ** -0.5).then_inc(
                            sem("exp_done"), 1)
                        if s == 0 and j == REP - 1 and not first:
                            act.activation(OT[:, U - 1], PS[:, 6], ACT.Copy).then_inc(sem("ot_done"), 1)
                        if s == CHAIN and j == REP - 1 and not last:
                            maxima(U + 1, 1 - par)
                    if last and s in (2, 5):
                        high_e(0, (s - 2) // 3, 4)
                    if s == 2 and par == 0 and q is not None:
                        act.wait_ge(sem("qs_loaded"), q * (2 * 16 * NTERM))
                        act.wait_ge(sem("finite_done"), q + len(EARLY))
                        high_part(0, QP[:, 0])
                    if s == 2 and par == 0 and q is not None:
                        middle_part(q + (len(EARLY) - 1), 0, QP[:, 1])

            attend(0, 0, True, False, None)
            attend(1, 1, False, False, None)
            act.wait_ge(sem("css_loaded"), 48)
            act.activation(CSS[:], CSA[:], ACT.Copy).then_inc(sem("css_done"), 1)
            with act.Fori(0, (PAIRS - 2) // 2) as i:
                for k in range(4):
                    attend(i * 4 + 2 + k, k % 2, False, False, i * 2 + 2 + k // 2 if k % 2 == 0 else None)
            attend(UNITS - 2, 0, False, False, None)
            attend(UNITS - 1, 1, False, True, None)
            act.wait_ge(sem("pv_done"), UNITS * TT)
            act.activation(OT[:, UNITS - 1], PS[:, 6], ACT.Copy).then_inc(sem("ot_done"), 1)

            for tick in range(EARLY_TICKS, TT + 8):
                t = tick - 7
                if 0 <= t < TT:
                    high_e(2, t, 0)
                t = tick - 5
                if 0 <= t < TT:
                    act.wait_ge(sem("rt_turned"), t + 1)
                    if t >= 1:
                        act.wait_ge(sem("cs_done"), t)
                    act.activation(RT[:], PS[0:3 * EXP, 1, P:2 * P], ACT.Copy).then_inc(sem("rt_done"), 1)
                t = tick - 4
                if 0 <= t < TT:
                    act.wait_ge(sem("lmax_done"), t + 1)
                    act.activation(RE[:], PS[:, 1, 0:EXP], ACT.Exp, bias=RM[:, 1:2],
                                   accum_out=RM[:, 2:3]).then_inc(sem("re_done"), 1)
                t = tick - 3
                if 0 <= t < TT:
                    high_e(1, t, 0)
                t = tick - 1
                if 0 <= t < TT:
                    high_e(0, t, 4)
                t = tick - 6
                if 0 <= t < TT:
                    act.wait_ge(sem("cs_done"), t + 1)
                    if t >= 3:
                        act.wait_ge(sem("zs_done"), t - 2)
                    act.activation(OS[:, t % 3], PS[:, 7], ACT.Copy).then_inc(sem("os_done"), 1)

        @block.vector
        def _(dve):
            dve.wait_ge(sem("m0_loaded"), 16)
            dve.tensor_reduce(BSUM[:], M0[:].rearrange("p k (b e) -> p (k b) e", e=32), AX, ALU.add).then_inc(
                sem("bsum_done"), 1)

            def stats(t0, t1):
                for q in range(t0 // 2, t1 // 2):
                    dve.wait_ge(sem(f"x_loaded{q}"), 16)
                    for t in (2 * q, 2 * q + 1):
                        dve.bn_stats(ST[:, t], X[:, t]).then_inc(sem("st_done"), 1)
                dve.wait_ge(sem("st_done"), t1)
                for t in range(t0, t1):
                    dve.bn_aggr(MV[:, t], ST[:, t]).then_inc(sem("ag_done"), 1)
                dve.wait_ge(sem("ag_done"), t1)
                dve.tensor_scalar(MV[:, t0:t1, 1], MV[:, t0:t1, 1], EPS, None, ALU.add).then_inc(sem("mv_done"), 1)

            stats(0, 2)
            dve.wait_ge(sem("block_sums"), 1)
            dve.tensor_scalar(BON[:], PS[:, 4, 0:KT * 16], 0.0, None, ALU.is_gt).then_inc(sem("bon_done"), 1)

            def mask_weight():
                dve.wait_ge(sem("bon_done"), 1)
                dve.wait_ge(sem("w0_loaded"), 16)
                for k in range(KT):
                    w = W0[:, k].rearrange("p (b e) -> p b e", e=32)
                    dve.tensor_tensor(w, w, BON[:, 16 * k:16 * k + 16].rearrange("p (b o) -> p b o", o=1).broadcast_to(
                        [P, 16, 32]), ALU.mult).then_inc(sem("w0m_done"), 1)

            def normalise(n, t, n_rstd):
                dve.wait_ge(sem("rstd_done"), n_rstd)
                if n >= 3:
                    dve.wait_ge(sem("tr_done"), n - 2)
                src = X[:, t].rearrange("p (C c h j) -> p C h c j", C=2, c=2, h=2)
                dst = XN[:, n % 3].rearrange("p (C h c j) -> p C h c j", C=2, c=2, h=2)
                for C in range(2):
                    ins = dve.tensor_scalar(dst[:, C], src[:, C], MV[:, t, 0:1], RSTD[:, t:t + 1],
                                            ALU.subtract, ALU.mult)
                    if C == 0:
                        ins.then_inc(sem("xn_half"), 1)
                    else:
                        ins.then_inc(sem("xn_done"), 1)

            def low(n):
                kind, t = order[n]
                dve.wait_ge(sem("xnh_done"), n + 1)
                dve.tensor_tensor(XNL[:, :, P * t:P * t + P], PS[:, n % 2].rearrange("p (k t) -> p k t", k=KT),
                                  f32(XNH[:, :, P * t:P * t + P]), ALU.subtract).then_inc(sem("xnl_done"), 1)

            def residual_stats(t, k):
                dve.wait_ge(sem("resid_done"), k + 1)
                dve.bn_stats(ST[:, t], X[:, t]).then_inc(sem("st_done"), 1)
                dve.wait_ge(sem("st_done"), TT + k + 1)
                dve.bn_aggr(MV[:, t], ST[:, t]).then_inc(sem("ag_done"), 1)
                dve.wait_ge(sem("ag_done"), TT + k + 1)
                dve.tensor_scalar(MV[:, t, 1:2], MV[:, t, 1:2], EPS, None, ALU.add).then_inc(sem("mv_done"), 1)

            def unpack13(h, par, first):
                dve.wait_ge(sem(f"p13_loaded{par}"), (h // 2 + 1) * 48)
                if not first:
                    dve.wait_ge(sem("wf_done"), h)
                dst = N13[:].rearrange("p (w b) o -> p w b o", b=2)
                dve.tensor_scalar(dst[:, :, 0], P13[:, par], 4, None, ALU.arith_shift_right).then_inc(
                    sem("n13_half"), 1)
                dve.tensor_scalar(dst[:, :, 1], P13[:, par], 28, 28, ALU.logical_shift_left,
                                  ALU.arith_shift_right).then_inc(sem("n13_done"), 1)
                dve.wait_ge(sem("n13_done"), h + 1)
                if not first:
                    dve.wait_ge(sem("wl_done"), h)
                    dve.wait_ge(sem("wh_done"), h)
                dve.tensor_tensor(WF[:], N13[:], S13[:, par], ALU.mult).then_inc(sem("wf_done"), 1)

            def unpack2(h, par, first):
                dve.wait_ge(sem(f"p2_loaded{par}"), (h // 2 + 1) * 80)
                if not first:
                    dve.wait_ge(sem("w2f_done"), h)
                for r in range(4):
                    ins = dve.tensor_scalar(N2[:].rearrange("p (v r) -> p r v", r=4)[:, r],
                                            P2[:, par].rearrange("p (v r) -> p r v", r=4)[:, r],
                                            SH2[:, r, 0:1], SH2[:, r, 1:2], ALU.logical_shift_left,
                                            ALU.arith_shift_right)
                    ins.then_inc(sem("n2_done") if r == 3 else sem("n2_part"), 1)
                dve.wait_ge(sem("n2_done"), h + 1)
                if not first:
                    dve.wait_ge(sem("w2l_done"), h)
                    dve.wait_ge(sem("w2h_done"), h)
                dve.tensor_tensor(W2F[:], N2[:], S2[:, par], ALU.mult).then_inc(sem("w2f_done"), 1)

            def unpack(h, par):
                unpack13(h, par, False)
                unpack2(h, par, False)

            normalise(0, 0, 1)
            normalise(1, 1, 1)
            mask_weight()
            low(0)
            low(1)
            stats(2, TT)
            dve.wait_ge(sem("id_loaded"), 16)
            dve.tensor_copy(IDB[:], ID[:]).then_inc(sem("idb_done"), 1)
            for t in range(TT):
                if t + 2 < TT:
                    normalise(seq[(1, t + 2)], t + 2, 2)
                dve.wait_ge(sem("y0_done"), t + 1)
                dve.wait_ge(sem("bias_done"), t + 1)
                dve.tensor_tensor(X[:, t], PS[:, 2 + t % 2], X[:, t], ALU.add).then_inc(sem("resid_done"), 1)
                residual_stats(t, t)
                if t >= 1:
                    low(seq[(2, t - 1)])
                if t + 2 < TT:
                    low(seq[(1, t + 2)])
                normalise(seq[(2, t)], t, 3 + t)
                if t == TT - 3:
                    unpack13(0, 0, True)
            unpack13(1, 1, False)
            unpack2(0, 0, True)
            low(seq[(2, TT - 1)])
            dve.wait_ge(sem("abs_used"), 6)
            dve.tensor_scalar(SQK[:], PS[:, 5, 0:5], 1.0 / DIM, 1e-8, ALU.mult, ALU.max).then_inc(sem("sc_done"), 1)
            dve.tensor_scalar(SVB[:], PS[:, 4, 0:P], 1.0 / DIM, 1e-8, ALU.mult, ALU.max).then_inc(sem("sc_done"), 1)
            dve.wait_ge(sem("sc_done"), 2)
            dve.tensor_tensor(SQK[:], SQK[:], QKSC[:], ALU.mult).then_inc(sem("sc_done"), 1)
            dve.tensor_tensor(SVB[:], SVB[:], VSC[:], ALU.mult).then_inc(sem("sc_done"), 1)

            def gate(n, h, c, pair, slot):
                dve.wait_ge(sem("th_done"), n + 1)
                if n >= 2:
                    dve.wait_ge(sem("hf_done"), n - 1)
                dve.scalar_tensor_tensor(UU[:, c], TH[:, c], 1.0, PS[:, 2 * pair], ALU.add, ALU.mult).then_inc(
                    sem("u_done"), 1)
                dve.wait_ge(sem("u_done"), n + 1)
                if n >= 2:
                    dve.wait_ge(sem("hh_done"), n - 1)
                    dve.wait_ge(sem("hl_done"), n - 1)
                dve.scalar_tensor_tensor(HF[:, c], UU[:, c], 0.5, PS[:, 2 * pair + 1], ALU.mult, ALU.mult).then_inc(
                    sem("hf_done"), 1)
                dve.wait_ge(sem("hh_done"), n + 1)
                dve.tensor_tensor(HL[:, slot, DIM * c:DIM * c + DIM], HF[:, c],
                                  f32(HH[:, slot, DIM * c:DIM * c + DIM]), ALU.subtract).then_inc(sem("hl_done"), 1)

            def low3(t):
                dve.wait_ge(sem("xnh3_done"), t + 1)
                dve.tensor_tensor(XNL[:, :, P * t:P * t + P], PS[:, 2 + t % 2].rearrange("p (k t) -> p k t", k=KT),
                                  f32(XNH[:, :, P * t:P * t + P]), ALU.subtract).then_inc(sem("xnl3_done"), 1)

            unpack2(1, 1, False)
            for half in range(2):
                h0, h1 = HALVES[half], HALVES[half + 1]
                for h in range(h0, h1):
                    for c in range(CH):
                        gate(2 * h + c, h, c, (2 * h + c + 3) % 4, h - h0)
                    if h + 2 < HT and h + 2 != h1 + 1:
                        unpack(h + 2, h % 2)
                for t in range(TT):
                    k = TT * (half + 1) + t
                    dve.wait_ge(sem("down_done"), TT * half + t + 1)
                    bank = t if half == 0 else 4 + t % 2
                    dve.tensor_tensor(X[:, t], PS[:, bank], X[:, t], ALU.add).then_inc(sem("resid_done"), 1)
                    if half:
                        dve.wait_ge(sem("resid_done"), k + 1)
                        dve.bn_stats(ST[:, t], X[:, t]).then_inc(sem("st_done"), 1)
                        dve.wait_ge(sem("st_done"), 2 * TT + t + 1)
                        dve.bn_aggr(MV[:, t], ST[:, t]).then_inc(sem("ag_done"), 1)
                        dve.wait_ge(sem("ag_done"), 2 * TT + t + 1)
                        dve.tensor_scalar(MV[:, t, 1:2], MV[:, t, 1:2], EPS, None, ALU.add).then_inc(sem("mv_done"), 1)
                        dve.wait_ge(sem("rstd_done"), 3 + TT + t)
                        n = t
                        if n >= 3:
                            dve.wait_ge(sem("tr3_done"), n - 2)
                        src = X[:, t].rearrange("p (C c h j) -> p C h c j", C=2, c=2, h=2)
                        dst = XN[:, n % 3].rearrange("p (C h c j) -> p C h c j", C=2, c=2, h=2)
                        for C in range(2):
                            ins = dve.tensor_scalar(dst[:, C], src[:, C], MV[:, t, 0:1], RSTD[:, t:t + 1],
                                                    ALU.subtract, ALU.mult)
                            ins.then_inc(sem("xn3_done") if C else sem("xn3_half"), 1)
                        if t >= 1:
                            low3(t - 1)
                if half == 0:
                    unpack(h1 + 1, (h1 + 1) % 2)
            low3(TT - 1)

            def finite(y, pos, neg, fin, name, k):
                dve.tensor_scalar(pos, y, 0.0, 1e6, ALU.max, ALU.min).then_inc(sem(name + "_step"), 1)
                dve.tensor_scalar(neg, y, 0.0, -1e6, ALU.min, ALU.max).then_inc(sem(name + "_step"), 1)
                if k:
                    dve.wait_ge(sem(name + "_done"), k)
                dve.tensor_scalar(fin, y, 0.0, 0.0, ALU.mult, ALU.is_equal).then_inc(sem(name + "_step"), 1)
                dve.wait_ge(sem(name + "_step"), 4 * k + 2)
                dve.tensor_tensor(pos, pos, neg, ALU.add).then_inc(sem(name + "_step"), 1)
                dve.wait_ge(sem(name + "_step"), 4 * k + 4)
                dve.copy_predicated(pos, fin.bitcast(I32), y).then_inc(sem(name + "_done"), 1)

            for u, (kind, c) in enumerate(EARLY):
                src = (kind, c, 0)
                dve.wait_ge(sem("ys_done"), PROJ.index(src) + 1)
                y = Y[:, slot_of(src)]
                if kind == "v":
                    y4 = y.rearrange("p (t o) -> p t o", t=QT)
                    dve.tensor_tensor(y4, y4, SVB[:].rearrange("p (t o) -> p t o", t=1).broadcast_to([P, QT, P]),
                                      ALU.mult).then_inc(sem("v_scaled"), 1)
                    dve.wait_ge(sem("v_scaled"), c + 1)
                if u >= 2:
                    dve.wait_ge(sem("split_done"), u - 1)
                finite(y, YP[:, u % 2], YN[:, u % 2], FIN[:], "finite", u)

            def row_max(n, par, i):
                dve.wait_ge(sem("score_done"), n + 1)
                b = 2 + 2 * (i % 2)
                dve.tensor_reduce(MX[:, par, i:i + 1], PS[:, b:b + 2], mybir.AxisListType.XY, ALU.max).then_inc(
                    sem("max_done"), 1)

            def minus_max(U, par):
                mx, nm = MX[:, par], NM[:, par]
                dve.wait_ge(sem("max_done"), (U + 1) * MAXT)
                dve.tensor_scalar(nm[:, 0], mx, -1.0, None, ALU.mult).then_inc(sem("nm_step"), 1)
                dve.wait_ge(sem("nm_step"), U * 3 + 1)
                dve.scalar_tensor_tensor(MR[:], mx, -1.0, nm[:, 0], ALU.mult, ALU.subtract).then_inc(sem("nm_step"), 1)
                dve.wait_ge(sem("nm_step"), U * 3 + 2)
                dve.tensor_copy(nm[:, 1], MR[:]).then_inc(sem("nm_step"), 1)
                dve.wait_ge(sem("nm_step"), U * 3 + 3)
                dve.tensor_tensor(nm[:, 2], MR[:], nm[:, 1], ALU.subtract).then_inc(sem("nm_done"), 1)

            def which_finite(q):
                dve.wait_ge(sem("yc_ready"), q)
                dve.tensor_scalar(FIN[:], YC, 0.0, 0.0, ALU.mult, ALU.is_equal).then_inc(sem("fin_done"), 1)

            def keep_finite():
                dve.copy_predicated(YP[:, 0], FIN[:].bitcast(I32), YC).then_inc(sem("finite_done"), 1)

            def maxima(U, par, q, left):
                for s in range(TT):
                    if s == 0 and par == 0 and q is not None:
                        which_finite(q)
                    if s == 1 and par == 0 and q is not None:
                        dve.wait_ge(sem("guarded"), q)
                    for e in range(2):
                        i = AHEAD + 2 * s + e
                        if i < left:
                            row_max(U * MAXT + MAXT + i, 1 - par if i < MAXT else par, i % MAXT)
                    if AHEAD + 2 * s + 2 == MAXT and left >= MAXT:
                        minus_max(U + 1, 1 - par)
                    if s == 1 and par == 0 and q is not None:
                        keep_finite()

            for n in range(MAXT + AHEAD):
                row_max(n, n // MAXT, n % MAXT)
                if n == MAXT - 1:
                    minus_max(0, 0)
                if n == MAXT // 2 - 2:
                    which_finite(1)
                    dve.wait_ge(sem("guarded"), 1)
                if n == MAXT // 2 + 1:
                    keep_finite()
            maxima(0, 0, None, 2 * MAXT)
            maxima(1, 1, None, 2 * MAXT)
            with dve.Fori(0, (PAIRS - 2) // 2) as i:
                for k in range(4):
                    maxima(i * 4 + 2 + k, k % 2, i * 2 + 2 + k // 2 if k % 2 == 0 else None, 2 * MAXT)
            maxima(UNITS - 2, 0, None, MAXT)

            def normal_o(t):
                dve.wait_ge(sem("to_done"), t + 1)
                o = PS[:, 2:4].rearrange("p b (h c) -> p (b h) c", c=32)
                dve.reciprocal(DEN[:], o[:, :, HD]).then_inc(sem("den_done"), 1)
                dve.wait_ge(sem("den_done"), t + 1)
                if t >= 2:
                    dve.wait_ge(sem("te0_done"), t - 1)
                dve.tensor_tensor(ON[:, t % 2].rearrange("p (h c) -> p h c", c=HD), o[:, :, 0:HD],
                                  DEN[:].rearrange("p (h o) -> p h o", o=1).broadcast_to([P, HEADS, HD]),
                                  ALU.mult).then_inc(sem("on_done"), 1)

            def low_e(kind, t, bank):
                dve.wait_ge(sem(f"he{kind}_done"), t + 1)
                dve.tensor_tensor(EL[:, kind, t % 2], PS[:, bank].rearrange("p (k t) -> p k t", k=KT),
                                  f32(EH[:, kind, t % 2]), ALU.subtract).then_inc(sem(f"le{kind}_done"), 1)

            for tick in range(TT + 8):
                t = tick - 8
                if 0 <= t < TT:
                    dve.wait_ge(sem("ue2_done"), t + 1)
                    if t >= 2:
                        dve.wait_ge(sem(f"stored{t % 2}"), 16 * (t // 2))
                    dve.tensor_tensor(ZO[:, t % 2], PS[:, 5], OS[:, t % 3], ALU.mult).then_inc(sem("zs_done"), 1)
                t = tick - 3
                if 0 <= t < TT:
                    dve.wait_ge(sem("rstd_done"), 3 + 2 * TT + t)
                    src = X[:, t].rearrange("p (C c h j) -> p C h c j", C=2, c=2, h=2)
                    dst = XE[:, t % 4].rearrange("p (C h c j) -> p C h c j", C=2, c=2, h=2)
                    for C in range(2):
                        dve.tensor_scalar(dst[:, C], src[:, C], MV[:, t, 0:1], RSTD[:, t:t + 1], ALU.subtract,
                                          ALU.mult).then_inc(sem("xe_done") if C else sem("xe_half"), 1)
                t = tick - 7
                if 0 <= t < TT:
                    low_e(2, t, 0)
                t = tick - 6
                if 0 <= t < TT:
                    dve.wait_ge(sem("cs_done"), t + 1)
                    dve.tensor_tensor(ZI[:, t % 2], PS[:, 6], XE[:, t % 4], ALU.mult).then_inc(sem("zi_done"), 1)
                t = tick - 4
                if 0 <= t < TT:
                    dve.wait_ge(sem("ue1_done"), t + 1)
                    dve.tensor_reduce(RM[:, 0:1], PS[:, 1, 0:EXP], AX, ALU.max).then_inc(sem("lm_step"), 1)
                    dve.wait_ge(sem("lm_step"), t + 1)
                    dve.tensor_scalar(RM[:, 1:2], RM[:, 0:1], -1.0, None, ALU.mult).then_inc(sem("lmax_done"), 1)
                t = tick - 4
                if 0 <= t < TT:
                    dve.wait_ge(sem("re_done"), t + 1)
                    dve.reciprocal(RM[:, 3:4], RM[:, 2:3]).then_inc(sem("r_step"), 1)
                    dve.wait_ge(sem("r_step"), 3 * t + 1)
                    dve.tensor_scalar(RF[:], RE[:], RM[:, 3:4], None, ALU.mult).then_inc(sem("r_step"), 1)
                    dve.wait_ge(sem("r_step"), 3 * t + 2)
                    if t >= 1:
                        dve.wait_ge(sem("rt_turned"), t)
                    dve.tensor_copy(RH[:], RF[:]).then_inc(sem("r_step"), 1)
                    dve.wait_ge(sem("r_step"), 3 * t + 3)
                    dve.tensor_copy(RL[:, 0:EXP], f32(RH[:])).then_inc(sem("rl_part"), 1)
                    dve.tensor_copy(RL[:, 2 * EXP:], f32(RH[:])).then_inc(sem("rl_part"), 1)
                    dve.tensor_tensor(RL[:, EXP:2 * EXP], RF[:], f32(RH[:]), ALU.subtract).then_inc(sem("rl_done"), 1)
                t = tick - 2
                if 0 <= t < TT:
                    dve.wait_ge(sem("ue0_done"), t + 1)
                    dve.tensor_tensor(EYS[:], PS[:, 5], SOB[:], ALU.mult).then_inc(sem("eys_done"), 1)
                    dve.wait_ge(sem("eys_done"), t + 1)
                    finite(EYS[:], EYP[:], EYN[:], EFIN[:], "efinite", t)
                    dve.wait_ge(sem("efinite_done"), t + 1)
                    dve.tensor_tensor(X[:, t], X[:, t], EYP[:], ALU.add).then_inc(sem("resid4_done"), 1)
                    dve.wait_ge(sem("resid4_done"), t + 1)
                    dve.bn_stats(ST[:, t], X[:, t]).then_inc(sem("st_done"), 1)
                    dve.wait_ge(sem("st_done"), 3 * TT + t + 1)
                    dve.bn_aggr(MV[:, t], ST[:, t]).then_inc(sem("ag_done"), 1)
                    dve.wait_ge(sem("ag_done"), 3 * TT + t + 1)
                    dve.tensor_scalar(MV[:, t, 1:2], MV[:, t, 1:2], EPS, None, ALU.add).then_inc(sem("mv_done"), 1)
                t = tick
                if t < TT:
                    normal_o(t)

        @block.tensor
        def _(pe):
            pe.wait_ge(sem("blk_loaded"), 16)
            pe.wait_ge(sem("bsum_done"), 1)
            pe.matmul(PS[:, 4, 0:KT * 16], BLK[:], BSUM[:], start=True, stop=True).then_inc(sem("block_sums"), 1)

            def transpose(n):
                pe.wait_ge(sem("xn_done"), n + 1)
                if n >= 2:
                    pe.wait_ge(sem("xnl_done"), n - 1)
                for k in range(KT):
                    ins = pe.transpose(PS[:, n % 2, P * k:P * k + P], XN[:, n % 3, P * k:P * k + P], ID[:])
                ins.then_inc(sem("tr_done"), 1)

            def three(dst, stat, mov, first, last):
                pe.matmul(dst, stat[0], mov[0], start=first, stop=False)
                pe.matmul(dst, stat[0], mov[1], start=False, stop=False)
                return pe.matmul(dst, stat[1], mov[0], start=False, stop=last)

            pe.wait_ge(sem("id_loaded"), 16)
            transpose(0)
            transpose(1)
            for t in range(TT):
                pe.wait_ge(sem("xnl_done"), seq[(1, t)] + 1)
                if t >= 2:
                    pe.wait_ge(sem("resid_done"), t - 1)
                ts = slice(P * t, P * t + P)
                for k in range(KT):
                    if t == 0:
                        pe.wait_ge(sem("w0l_done"), k + 1)
                    ins = three(PS[:, 2 + t % 2], (XNH[:, k, ts], XNL[:, k, ts]), (W0H[:, k], W0L[:, k]),
                                k == 0, k == KT - 1)
                ins.then_inc(sem("y0_done"), 1)
                if t >= 1:
                    transpose(seq[(2, t - 1)])
                if t + 2 < TT:
                    transpose(seq[(1, t + 2)])
                if t == 0:
                    pe.wait_ge(sem("consts_loaded"), 16 * 5)
                if 1 <= t < 7:
                    n = t - 1
                    pe.wait_ge(sem("abs_done"), n + 1)
                    a = ABS[:, n % 2]
                    if n < 4:
                        for T in range(4):
                            ins = pe.matmul(PS[:, 5, T:T + 1], a[:, P * T:P * T + P], ONES[:, 0:1],
                                            start=(n == 0 and T == 0), stop=(n == 3), skip_group_check=True)
                    else:
                        for kk in range(2):
                            b = a[:, 2 * P * kk:2 * P * kk + 2 * P]
                            pe.matmul(PS[:, 5, 4:5], b[:, 0:P], ONES[:, 0:1], start=False,
                                      stop=(n == 5 and kk == 1), skip_group_check=True)
                            ins = pe.matmul(PS[:, 4, 0:P], ONES[:], b[:, P:2 * P], start=(n == 4 and kk == 0),
                                            stop=(n == 5 and kk == 1))
                    ins.then_inc(sem("abs_used"), 1)
            for half in range(2):
                h0, h1 = HALVES[half], HALVES[half + 1]
                for h in range(h0, h1):
                    par = h % 2
                    pe.wait_ge(sem("wl_done"), h + 1)
                    for c in range(CH):
                        n = 2 * h + c
                        pair = (n + 3) % 4
                        if n == 0:
                            pe.wait_ge(sem("xnl_done"), seq[(2, QT - 1)] + 1)
                        if n == 1:
                            pe.wait_ge(sem("xnl_done"), NA)
                        if n == 2:
                            pe.wait_ge(sem("resid_done"), TT)
                        if n == 3:
                            pe.wait_ge(sem("sc_done"), 4)
                        if n >= 4:
                            pe.wait_ge(sem("hf_done"), n - 3)
                        if half and n < 2 * h0 + 4:
                            pe.wait_ge(sem("resid_done"), TT + 2 * pair + 2)
                        cs = slice(DIM * c, DIM * c + DIM)
                        for w in range(2):
                            if n == 0 and w == 1:
                                transpose(seq[(2, TT - 1)])
                            for k in range(KT):
                                ins = three(PS[:, 2 * pair + w], (WH[:, par, w, k], WL[:, par, w, k]),
                                            (XNH[:, k, cs], XNL[:, k, cs]), k == 0, k == KT - 1)
                        ins.then_inc(sem("up_done"), 1)
                for t in range(TT):
                    ts = slice(P * t, P * t + P)
                    bank = t if half == 0 else 4 + t % 2
                    if half and t >= 2:
                        pe.wait_ge(sem("resid_done"), 2 * TT + t - 1)
                    if half == 0 and t % 2 == 0:
                        pe.wait_ge(sem("hf_done"), 2 * h1 - 3 + (t // 2 + 1) % 4)
                    if half and t == 0:
                        pe.wait_ge(sem("hf_done"), 2 * h1 - 2)
                    for s in range(h1 - h0):
                        if t % QT == 0:
                            pe.wait_ge(sem("hl_done"), 2 * (h0 + s) + 1 + t // QT)
                        if t == 0:
                            pe.wait_ge(sem("w2l_done"), h0 + s + 1)
                        ins = three(PS[:, bank], (HH[:, s, ts], HL[:, s, ts]), (W2H[:, s], W2L[:, s]),
                                    s == 0, s == h1 - h0 - 1)
                    ins.then_inc(sem("down_done"), 1)
                    if half and t >= 1:
                        transpose3(pe, t - 1)
                if half:
                    def project(u):
                        kind, c, T = PROJ[u]
                        bank = PBANK[u % 4]
                        if u >= 4:
                            pe.wait_ge(sem("ys_done"), u - 3)
                        cs = slice(DIM * c, DIM * c + DIM)
                        if kind == "v":
                            for tt in range(QT):
                                ts = slice(DIM * c + P * tt, DIM * c + P * tt + P)
                                for k in range(KT):
                                    for x in (XNH, XNL):
                                        ins = pe.matmul(PS[:, bank, P * tt:P * tt + P], x[:, k, ts],
                                                        SGKV[:, k, P:2 * P], start=(k == 0 and x is XNH),
                                                        stop=(k == KT - 1 and x is XNL))
                        else:
                            for k in range(KT):
                                w = SGKV[:, k, 0:P] if kind == "k" else SGQ[:, k, P * T:P * T + P]
                                for x in (XNH, XNL):
                                    ins = pe.matmul(PS[:, bank], w, x[:, k, cs], start=(k == 0 and x is XNH),
                                                    stop=(k == KT - 1 and x is XNL))
                        ins.then_inc(sem("proj_done"), 1)

                    pe.wait_ge(sem("xnl3_done"), 4)
                    for u in range(3):
                        project(u)
                    transpose3(pe, TT - 1)
                    for u in range(3, 6):
                        project(u)
                    pe.wait_ge(sem("xnl3_done"), TT)
                    for u in range(6, len(PROJ)):
                        project(u)

            def score_rows(n, slot, g, i, first):
                b = 2 + 2 * (i % 2)
                if not first:
                    pe.wait_ge(sem("max_done"), n - 1)
                j, qt = i // QT, i % QT
                for c in range(CH):
                    ins = pe.matmul(PS[:, b + c], QS[0:SROWS, slot, j, P * qt:P * qt + P],
                                    KS[0:SROWS, g, DIM * c:DIM * c + DIM], start=True, stop=True)
                ins.then_inc(sem("score_done"), 1)

            def maxima(par):
                pe.transpose(PS[0:3 * MAXT, KEYBANK[2], 0:P // 2].bitcast(BF16), NM[:, par].rearrange("p a i -> p (a i)"),
                             IDB[:]).then_inc(sem("nmt_done"), 1)

            def score_cols(U, s, j, first=False):
                n = U * (TT * REP) + s * REP + j
                if s == 0 and j == 0:
                    pe.wait_ge(sem("m_loaded"), U * 16 + 16)
                if not first:
                    pe.wait_ge(sem("exp_done"), n - BEHIND[j])
                pe.matmul(PS[:, KEYBANK[j]], KS[0:MROWS, U & (KVH - 1), P * s:P * s + P],
                          QS[0:MROWS, U & (RING - 1), j], start=True, stop=True).then_inc(sem("keyscore_done"), 1)

            def weigh(U, par, s, first):
                pe.wait_ge(sem("exp_done"), U * (TT * REP) + REP * (s + 1))
                if s == 0:
                    pe.wait_ge(sem("vs_done"), U + 1)
                    if not first:
                        pe.wait_ge(sem("ot_done"), U)
                for j in range(REP):
                    ins = pe.matmul(PS[32 * j:32 * j + 32, 6], VS[:, par, s], PR[:, s % 2, j], start=(s == 0),
                                    stop=(s == TT - 1), tile_position=(0, 32 * j))
                ins.then_inc(sem("pv_done"), 1)

            def turn_o(t):
                if t == 0:
                    pe.wait_ge(sem("max_done"), UNITS * MAXT)
                if t % QT == 0:
                    pe.wait_ge(sem("ot_done"), KVH * (t // QT + 1))
                if t >= 1:
                    pe.wait_ge(sem("on_done"), t)
                for g in range(KVH):
                    ins = pe.transpose(PS[:, 2 + g // 4, P * (g % 4):P * (g % 4) + P],
                                       OT[:, KVH * (t // QT) + g, P * (t % QT):P * (t % QT) + P], ID[:])
                ins.then_inc(sem("to_done"), 1)

            def turn(kind, t, src, bank):
                for k in range(KT):
                    ins = pe.transpose(PS[:, bank, P * k:P * k + P], src[:, P * k:P * k + P], ID[:])
                ins.then_inc(sem(f"te{kind}_done"), 1)

            def by_signs(kind, t, w, bank):
                pe.wait_ge(sem(f"le{kind}_done"), t + 1)
                for k in range(KT):
                    pe.matmul(PS[:, bank], EH[:, kind, t % 2, k], w[:, k], start=(k == 0), stop=False)
                    ins = pe.matmul(PS[:, bank], EL[:, kind, t % 2, k], w[:, k], start=False, stop=(k == KT - 1))
                ins.then_inc(sem(f"ue{kind}_done"), 1)

            def end_tick(tick):
                t = tick - 8
                if 0 <= t < TT:
                    if t == 0:
                        pe.wait_ge(sem("sgf_done"), 1)
                    pe.wait_ge(sem("eys_done"), min(t + 6, TT))
                    if t >= 1:
                        pe.wait_ge(sem("zs_done"), t)
                    by_signs(2, t, SGF, 5)
                t = tick - 7
                if 0 <= t < TT:
                    pe.wait_ge(sem("zi_done"), t + 1)
                    pe.wait_ge(sem("he1_done"), min(t + 4, TT))
                    turn(2, t, ZI[:, t % 2], 0)
                t = tick - 6
                if 0 <= t < TT:
                    pe.wait_ge(sem("rt_done"), t + 1)
                    if t == 0:
                        pe.wait_ge(sem("css_done"), 1)
                    else:
                        pe.wait_ge(sem("zi_done"), t)
                        pe.wait_ge(sem("os_done"), t)
                    pe.matmul(PS[:, 6], RT[:], CSS[:, 0:DIM], start=True, stop=True)
                    pe.matmul(PS[:, 7], RT[:], CSS[:, DIM:], start=True, stop=True).then_inc(sem("cs_done"), 1)
                t = tick - 5
                if 0 <= t < TT:
                    pe.wait_ge(sem("rl_done"), t + 1)
                    pe.transpose(PS[0:3 * EXP, 1, P:2 * P], RL[:], ID[:]).then_inc(sem("rt_turned"), 1)
                t = tick - 4
                if 0 <= t < TT:
                    pe.wait_ge(sem("le1_done"), t + 1)
                    if t == 0:
                        pe.wait_ge(sem("gate_split"), 2)
                    else:
                        pe.wait_ge(sem("rt_done"), t)
                    for k in range(KT):
                        ins = three(PS[:, 1, 0:EXP], (EH[:, 1, t % 2, k], EL[:, 1, t % 2, k]), (GTH[:, k], GTL[:, k]),
                                    k == 0, k == KT - 1)
                    ins.then_inc(sem("ue1_done"), 1)
                t = tick - 2
                if 0 <= t < TT:
                    if t == 0:
                        pe.wait_ge(sem("sgo_done"), 1)
                        pe.wait_ge(sem("sob_done"), 2)
                    if t >= 6:
                        pe.wait_ge(sem("zs_done"), t - 5)
                    by_signs(0, t, SGO, 5)
                t = tick - 1
                if 0 <= t < TT:
                    pe.wait_ge(sem("on_done"), t + 1)
                    if t >= 1:
                        pe.wait_ge(sem("he0_done"), t)
                    turn(0, t, ON[:, t % 2], 4)
                t = tick - 3
                if 0 <= t < TT:
                    pe.wait_ge(sem("xe_done"), t + 1)
                    if t >= 1:
                        pe.wait_ge(sem("he1_done"), t)
                    if t >= 4:
                        pe.wait_ge(sem("le2_done"), t - 3)
                    turn(1, t, XE[:, t % 4], 0)
                t = tick
                if t < TT:
                    turn_o(t)

            def attend(U, par, first, last, left):
                for s in range(TT):
                    def cols(j):
                        if s + 1 < TT:
                            score_cols(U, s + 1, j)
                        elif not last:
                            score_cols(U + 1, 0, j)

                    def rows(e):
                        i = AHEAD + 2 * s + e
                        if i < left:
                            V = U + 1 if i < MAXT else U + 2
                            if i == MAXT:
                                pe.wait_ge(sem("qs_loaded"), V * (16 * NTERM) + 16 * NTERM)
                            score_rows(U * MAXT + MAXT + i, V & (RING - 1), V & (KVH - 1), i % MAXT, False)

                    turning = s == CHAIN and left >= MAXT
                    cols(0)
                    rows(0)
                    if turning:
                        pe.wait_ge(sem("nm_done"), U + 2)
                    cols(1)
                    if turning:
                        maxima(1 - par)
                    else:
                        cols(2)
                    weigh(U, par, s, first)
                    if turning:
                        pe.wait_ge(sem("mt_done"), U + 2)
                        cols(2)
                    cols(3)
                    rows(1)
                    if isinstance(U, int) and (U, s) in TICK_AT:
                        end_tick(TICK_AT.index((U, s)))

            pe.wait_ge(sem("idb_done"), 1)
            pe.wait_ge(sem("ys_done"), len(PROJ))
            pe.wait_ge(sem("qs_loaded"), 16 * NTERM)
            pe.wait_ge(sem("ks_loaded"), 16 * NTERM * CH)
            for n in range(MAXT + AHEAD):
                if n == MAXT:
                    pe.wait_ge(sem("qs_loaded"), 16 * NTERM * 2)
                score_rows(n, n // MAXT, n // MAXT, n % MAXT, n < 2)
                if n >= MAXT and n % 2 == 0:
                    k = (n - MAXT) // 2
                    if k == 0:
                        pe.wait_ge(sem("abso_done"), 1)
                    ins = pe.matmul(PS[:, 6], ONES[:], RAWO[:, k], start=(k == 0), stop=(k == KT - 1))
                    if k == KT - 1:
                        ins.then_inc(sem("abso_sums"), 1)
                if n == MAXT + 1:
                    pe.wait_ge(sem("nm_done"), 1)
                    maxima(0)
            pe.wait_ge(sem("mt_done"), 1)
            pe.wait_ge(sem("ks_ones"), 1)
            for j in range(REP):
                score_cols(0, 0, j, j < 3)
            pe.wait_ge(sem("sob_means"), 1)
            attend(0, 0, True, False, 2 * MAXT)
            attend(1, 1, False, False, 2 * MAXT)
            with pe.Fori(0, (PAIRS - 2) // 2) as i:
                for k in range(4):
                    attend(i * 4 + 2 + k, k % 2, False, False, 2 * MAXT)
            attend(UNITS - 2, 0, False, False, MAXT)
            attend(UNITS - 1, 1, False, True, 0)

            for tick in range(EARLY_TICKS, TT + 8):
                end_tick(tick)



def layout(inp):
    import numpy as np
    g = {k: np.ascontiguousarray(v) for k, v in inp.items()}

    def contraction(wT):
        n = wT.shape[1]
        return wT.reshape(2, 2, 2, 64, n).transpose(1, 3, 0, 2, 4).reshape(P, KT, n)

    def rows(a):
        return a.reshape(1, -1)

    pad = HT * P - HID

    def packed(w):
        w = np.concatenate([w.reshape(HID, 2, 2, 64), np.zeros((pad, 2, 2, 64), w.dtype)])
        return w.reshape(HT, P, 2, 2, 64).transpose(0, 3, 4, 2, 1).reshape(HT, P, 2, P)

    def scales(s):
        s = np.concatenate([s.reshape(HID, 2, 2, 2), np.zeros((pad, 2, 2, 2), s.dtype)])
        return s.reshape(HT, P, 2, 2, 2).transpose(0, 3, 2, 4, 1).reshape(HT, 2, 4, P)

    flat = np.arange(DIM * HID).reshape(DIM, HID)
    w2 = g["L0_ffn_w2"][flat // 128, flat % 64].T
    w2 = np.concatenate([w2, np.zeros((pad, DIM), w2.dtype)]).reshape(HT, P, DIM)
    s2 = g["L0_ffn_s2"][flat[:, ::32] // 64].T
    s2 = np.concatenate([s2, np.zeros((pad // 32, DIM), s2.dtype)]).reshape(HT, 4, DIM)
    half2 = (96 * np.arange(4)[None] + np.arange(P)[:, None]) % 128 // 64

    def stacked(a, heads):
        return a.reshape(-1, heads, HD, *a.shape[1:]).swapaxes(1, 2).reshape(a.shape)

    wq = contraction(stacked(g["L1_attn_q_weight"], REP).T)
    wkv = contraction(np.concatenate([stacked(g["L1_attn_k_weight"], KVH), g["L1_attn_v_weight"]]).T)
    qkv = np.concatenate([wq.transpose(1, 0, 2), wkv.reshape(P, 2, DIM).transpose(1, 0, 2)])
    return {
        "x": g["L0_attn_data"].reshape(TT, P, DIM).transpose(1, 0, 2),
        "m0": contraction(g["L0_attn_mask"].T),
        "w0": contraction(g["L0_attn_weight"].T),
        "bias0": rows(g["L0_attn_bias"]),
        "p13": np.concatenate([packed(g["L0_ffn_w1"]), packed(g["L0_ffn_w3"])], axis=2),
        "s13": np.concatenate([scales(g["L0_ffn_s1"]), scales(g["L0_ffn_s3"])], axis=2),
        "p2": w2,
        "s2": s2,
        "sh2": np.stack([28 * half2, 4 + 24 * half2], axis=2).astype(np.int32),
        "wqkv": qkv,
        "qksc": np.concatenate([stacked(g["L1_attn_q_scale"], REP).reshape(4, P),
                                stacked(g["L1_attn_k_scale"], KVH).reshape(1, P)]).T,
        "vsc": rows(g["L1_attn_v_scale"]),
        "wo": g["L1_attn_o_weight"].T.reshape(KT, P, DIM).transpose(1, 0, 2),
        "osc": rows(g["L1_attn_o_scale"]),
        "wf": contraction(g["L1_ffn_weight"].T),
        "biasf": rows(g["L1_ffn_bias"]),
        "gate": contraction(g["L1_ffn_gate_w"].T),
        "cs": np.concatenate([g["L1_ffn_in_channel_scale"].reshape(EXP, 2, 2, 2, 64).transpose(0, 1, 3, 2, 4)
                              .reshape(EXP, DIM), g["L1_ffn_out_channel_scale"]], axis=1),
        "ident": np.eye(P, dtype=np.float32),
        "ones": np.ones((P, P), np.float32),
        "blk": np.kron(np.eye(4), np.ones((32, 32))).astype(np.float32),
    }


def kernel(**inputs):
    import numpy as np
    from concourse import bacc
    from concourse.bass_utils import run_bass_kernel_spmd

    arrays = {f"in_{k}": np.ascontiguousarray(v) for k, v in layout(inputs).items()}
    nc = bacc.Bacc("TRN2", target_bir_lowering=False, num_devices=1)
    A = {k[3:]: nc.dram_tensor(k, v.shape, mybir.dt.from_np(v.dtype), kind="ExternalInput").ap()
         for k, v in arrays.items()}
    out = nc.dram_tensor("out", (P, TT, DIM), F32, kind="ExternalOutput").ap()
    build(nc, A, out)
    r = run_bass_kernel_spmd(nc, [arrays], core_ids=[0])
    return r.results[0]["out"].transpose(1, 0, 2).reshape(1, TOK, DIM)
```
